# Optimizing a Trainium2 kernel written in Bass

```python
import numpy as np
import jax
import jax.numpy as jnp

def _softmax(x, axis=-1):
    return jax.nn.softmax(x, axis=axis)

def _gelu(x):
    return jax.nn.gelu(x, approximate=True)

def _silu(x):
    return jax.nn.silu(x)

def _sigmoid(x):
    return jax.nn.sigmoid(x)

def _layernorm(x, axis=-1, eps=1e-05):
    m = jnp.mean(x, axis=axis, keepdims=True)
    v = jnp.var(x, axis=axis, keepdims=True)
    return (x - m) / jnp.sqrt(v + eps)

def _scatter_add(tgt, idx, src, axis=0):
    return tgt.at[idx].add(src)

def _segment_sum(src, seg, n):
    return jax.ops.segment_sum(src, seg, n)
kernel_name = 'mk_gnn_resnorm_d4_gnn_r32_ef7bf1'

def setup_inputs(seed: int=0):
    np.random.seed(seed)
    _w = jnp.asarray

    def _rec_inputs():
        import jax
        import jax.numpy as jnp
        _gk = jax.random.key(seed)
        x = -0.000202 + 1 * jax.random.normal(jax.random.fold_in(_gk, 1), (3125, 64), jnp.float32)
        _s = jax.random.randint(jax.random.fold_in(_gk, 2), (50000,), 0, 3125, jnp.int32)
        _d = jax.random.randint(jax.random.fold_in(_gk, 3), (50000,), 0, 3125, jnp.int32)
        _loop = jnp.arange(3125, dtype=jnp.int32)
        src = jnp.concatenate([_s, _d, _loop])
        dst = jnp.concatenate([_d, _s, _loop])
        _o = jnp.argsort(dst, stable=True)
        src = src[_o]
        dst = dst[_o]
        edge_attr_32 = 0.000196303 + 1.00016 * jax.random.normal(jax.random.fold_in(_gk, 12), (103125, 32), jnp.float32)
        edge_type_16 = jax.random.randint(jax.random.fold_in(_gk, 14), (103125,), 0, 16, jnp.int32)
        edge_weight1 = jax.random.uniform(jax.random.fold_in(_gk, 15), (103125, 1), jnp.float32, 0.0, 1)
        return (x, src, dst, edge_attr_32, edge_type_16, edge_weight1)
    x, src, dst, edge_attr_32, edge_type_16, edge_weight1 = _rec_inputs()

    def _L0_gnn_setup():
        import jax, jax.numpy as jnp
        import numpy as np
        N_NODES = 3125
        N_EDGES = 50000
        D_FEAT = 64
        key = jax.random.key(seed)
        k1, k2 = jax.random.split(key)
        x = jax.random.normal(k1, (N_NODES, D_FEAT), dtype=jnp.float32)
        edge_index = jax.random.randint(k2, (2, N_EDGES), 0, N_NODES, dtype=jnp.int64)
        return {'x': x, 'edge_index': edge_index}
    _L0_gnn_all = _L0_gnn_setup()
    _L0_gnn_in = {k: v for k, v in _L0_gnn_all.items() if k in ()}
    del _L0_gnn_all

    def _L1_gnn_setup():
        import jax, jax.numpy as jnp
        import numpy as np
        N = 50000
        E = 25000
        D = 64
        H = 64
        DE = 32

        def _transformer_conv(x, src, dst, edge_attr, wq, bq, wk, bk, wv, bv, we, ws, bs, n_nodes):
            q = x @ wq + bq
            k = x @ wk + bk
            v = x @ wv + bv
            e = edge_attr @ we
            ke = k[src] + e
            score = jnp.sum(q[dst] * ke, axis=-1) / jnp.sqrt(jnp.asarray(ke.shape[-1], x.dtype))
            smax = jax.ops.segment_max(score, dst, num_segments=n_nodes)
            a = jnp.exp(score - smax[dst])
            denom = jax.ops.segment_sum(a, dst, num_segments=n_nodes)
            alpha = a / denom[dst]
            msg = alpha[:, None] * (v[src] + e)
            out = jax.ops.segment_sum(msg, dst, num_segments=n_nodes)
            out = out + x @ ws + bs
            return out
        key = jax.random.key(seed)
        ks = jax.random.split(key, 24)

        def g(i, shape, scale):
            return jax.random.normal(ks[i], shape, dtype=jnp.float32) * scale
        inp = {'x': g(0, (N, D), 1.0), 'edge_index': jax.random.randint(ks[1], (2, E), 0, N, dtype=jnp.int64), 'edge_attr': g(2, (E, DE), 1.0), 'q1_w': g(3, (D, H), D ** (-0.5)), 'q1_b': jnp.zeros((H,), jnp.float32), 'k1_w': g(4, (D, H), D ** (-0.5)), 'k1_b': jnp.zeros((H,), jnp.float32), 'v1_w': g(5, (D, H), D ** (-0.5)), 'v1_b': jnp.zeros((H,), jnp.float32), 'e1_w': g(6, (DE, H), DE ** (-0.5)), 's1_w': g(7, (D, H), D ** (-0.5)), 's1_b': jnp.zeros((H,), jnp.float32), 'q2_w': g(8, (H, H), H ** (-0.5)), 'q2_b': jnp.zeros((H,), jnp.float32), 'k2_w': g(9, (H, H), H ** (-0.5)), 'k2_b': jnp.zeros((H,), jnp.float32), 'v2_w': g(10, (H, H), H ** (-0.5)), 'v2_b': jnp.zeros((H,), jnp.float32), 'e2_w': g(11, (DE, H), DE ** (-0.5)), 's2_w': g(12, (H, H), H ** (-0.5)), 's2_b': jnp.zeros((H,), jnp.float32), 'skip_w': g(13, (2 * H, D), (2 * H) ** (-0.5)), 'skip_b': jnp.zeros((D,), jnp.float32)}
        return inp
    _L1_gnn_all = _L1_gnn_setup()
    _L1_gnn_in = {k: v for k, v in _L1_gnn_all.items() if k in ('q1_w', 'q1_b', 'k1_w', 'k1_b', 'v1_w', 'v1_b', 'e1_w', 's1_w', 's1_b', 'q2_w', 'q2_b', 'k2_w', 'k2_b', 'v2_w', 'v2_b', 'e2_w', 's2_w', 's2_b', 'skip_w', 'skip_b')}
    del _L1_gnn_all

    def _L2_gnn_setup():
        import jax, jax.numpy as jnp
        import numpy as np
        N_NODES = 3125
        N_EDGES = 100000
        IN_FEAT = 64
        OUT_FEAT = 64
        NUM_RELS = 16
        key = jax.random.key(seed)
        k1, k2, k3, k4, k5, k6 = jax.random.split(key, 6)
        h = jax.random.normal(k1, (N_NODES, IN_FEAT), dtype=jnp.float32)
        weight = jax.random.normal(k2, (NUM_RELS, IN_FEAT, OUT_FEAT), dtype=jnp.float32) * 0.1
        norm = jax.random.uniform(k3, (N_EDGES, 1), dtype=jnp.float32)
        src = jax.random.randint(k4, (N_EDGES,), 0, N_NODES, dtype=jnp.int32)
        dst = jax.random.randint(k5, (N_EDGES,), 0, N_NODES, dtype=jnp.int32)
        rel_type = jax.random.randint(k6, (N_EDGES,), 0, NUM_RELS, dtype=jnp.int32)
        return {'h': h, 'weight': weight, 'norm': norm, 'src': src, 'dst': dst, 'rel_type': rel_type}
    _L2_gnn_all = _L2_gnn_setup()
    _L2_gnn_in = {k: v for k, v in _L2_gnn_all.items() if k in ('weight',)}
    del _L2_gnn_all

    def _L3_gnn_setup():
        import jax, jax.numpy as jnp
        import numpy as np
        N_NODES = 50000
        N_EDGES = 25000
        FEAT = 64
        N_LAYERS = 3

        def _edgeconv(x, src, dst, W1, b1, W2, b2):
            xi = x[dst]
            xj = x[src]
            m = jnp.concatenate([xi, xj - xi], axis=-1)
            h = jax.nn.relu(m @ W1 + b1)
            h = h @ W2 + b2
            out = jax.ops.segment_max(h, dst, num_segments=x.shape[0])
            return jnp.where(jnp.isfinite(out), out, 0.0)
        key = jax.random.key(seed)
        ks = jax.random.split(key, 6)
        x = jax.random.normal(ks[0], (N_NODES, FEAT), dtype=jnp.float32)
        edge_index = jax.random.randint(ks[1], (2, N_EDGES), 0, N_NODES, dtype=jnp.int64)
        s = 1.0 / np.sqrt(2 * FEAT)
        W1 = jax.random.uniform(ks[2], (N_LAYERS, 2 * FEAT, FEAT), jnp.float32, -s, s)
        b1 = jax.random.uniform(ks[3], (N_LAYERS, FEAT), jnp.float32, -s, s)
        s2 = 1.0 / np.sqrt(FEAT)
        W2 = jax.random.uniform(ks[4], (N_LAYERS, FEAT, FEAT), jnp.float32, -s2, s2)
        b2 = jax.random.uniform(ks[5], (N_LAYERS, FEAT), jnp.float32, -s2, s2)
        return {'x': x, 'edge_index': edge_index, 'W1': W1, 'b1': b1, 'W2': W2, 'b2': b2}
    _L3_gnn_all = _L3_gnn_setup()
    _L3_gnn_in = {k: v for k, v in _L3_gnn_all.items() if k in ('W1', 'b1', 'W2', 'b2')}
    del _L3_gnn_all
    return {'x': x, 'src': src, 'dst': dst, 'edge_attr_32': edge_attr_32, 'edge_type_16': edge_type_16, 'edge_weight1': edge_weight1, 'L1_gnn_q1_w': _L1_gnn_in['q1_w'], 'L1_gnn_q1_b': _L1_gnn_in['q1_b'], 'L1_gnn_k1_w': _L1_gnn_in['k1_w'], 'L1_gnn_k1_b': _L1_gnn_in['k1_b'], 'L1_gnn_v1_w': _L1_gnn_in['v1_w'], 'L1_gnn_v1_b': _L1_gnn_in['v1_b'], 'L1_gnn_e1_w': _L1_gnn_in['e1_w'], 'L1_gnn_s1_w': _L1_gnn_in['s1_w'], 'L1_gnn_s1_b': _L1_gnn_in['s1_b'], 'L1_gnn_q2_w': _L1_gnn_in['q2_w'], 'L1_gnn_q2_b': _L1_gnn_in['q2_b'], 'L1_gnn_k2_w': _L1_gnn_in['k2_w'], 'L1_gnn_k2_b': _L1_gnn_in['k2_b'], 'L1_gnn_v2_w': _L1_gnn_in['v2_w'], 'L1_gnn_v2_b': _L1_gnn_in['v2_b'], 'L1_gnn_e2_w': _L1_gnn_in['e2_w'], 'L1_gnn_s2_w': _L1_gnn_in['s2_w'], 'L1_gnn_s2_b': _L1_gnn_in['s2_b'], 'L1_gnn_skip_w': _L1_gnn_in['skip_w'], 'L1_gnn_skip_b': _L1_gnn_in['skip_b'], 'L2_gnn_weight': _L2_gnn_in['weight'], 'L3_gnn_W1': _L3_gnn_in['W1'], 'L3_gnn_b1': _L3_gnn_in['b1'], 'L3_gnn_W2': _L3_gnn_in['W2'], 'L3_gnn_b2': _L3_gnn_in['b2']}

def reference(x, src, dst, edge_attr_32, edge_type_16, edge_weight1, L1_gnn_q1_w, L1_gnn_q1_b, L1_gnn_k1_w, L1_gnn_k1_b, L1_gnn_v1_w, L1_gnn_v1_b, L1_gnn_e1_w, L1_gnn_s1_w, L1_gnn_s1_b, L1_gnn_q2_w, L1_gnn_q2_b, L1_gnn_k2_w, L1_gnn_k2_b, L1_gnn_v2_w, L1_gnn_v2_b, L1_gnn_e2_w, L1_gnn_s2_w, L1_gnn_s2_b, L1_gnn_skip_w, L1_gnn_skip_b, L2_gnn_weight, L3_gnn_W1, L3_gnn_b1, L3_gnn_W2, L3_gnn_b2):
    import jax
    import jax.numpy as jnp

    def _L0_gnn_ref(x, edge_index):
        import jax, jax.numpy as jnp
        import numpy as np
        N_NODES = 3125
        N_EDGES = 50000
        D_FEAT = 64
        from_, to_ = (edge_index[0], edge_index[1])
        n = x.shape[0]
        deg = jax.ops.segment_sum(jnp.ones_like(to_, dtype=x.dtype), to_, num_segments=n)
        deg_inv = jnp.where(deg > 0, 1.0 / jnp.sqrt(deg), 0.0)
        norm = deg_inv[from_] * deg_inv[to_]
        m_j = norm[:, None] * x[from_]
        out = jax.ops.segment_sum(m_j, to_, num_segments=n)
        return out

    def _L1_gnn_ref(x, edge_index, edge_attr, q1_w, q1_b, k1_w, k1_b, v1_w, v1_b, e1_w, s1_w, s1_b, q2_w, q2_b, k2_w, k2_b, v2_w, v2_b, e2_w, s2_w, s2_b, skip_w, skip_b):
        import jax, jax.numpy as jnp
        import numpy as np
        N = 50000
        E = 25000
        D = 64
        H = 64
        DE = 32

        def _transformer_conv(x, src, dst, edge_attr, wq, bq, wk, bk, wv, bv, we, ws, bs, n_nodes):
            q = x @ wq + bq
            k = x @ wk + bk
            v = x @ wv + bv
            e = edge_attr @ we
            ke = k[src] + e
            score = jnp.sum(q[dst] * ke, axis=-1) / jnp.sqrt(jnp.asarray(ke.shape[-1], x.dtype))
            smax = jax.ops.segment_max(score, dst, num_segments=n_nodes)
            a = jnp.exp(score - smax[dst])
            denom = jax.ops.segment_sum(a, dst, num_segments=n_nodes)
            alpha = a / denom[dst]
            msg = alpha[:, None] * (v[src] + e)
            out = jax.ops.segment_sum(msg, dst, num_segments=n_nodes)
            out = out + x @ ws + bs
            return out
        src, dst = (edge_index[0], edge_index[1])
        n = x.shape[0]
        h1 = jax.nn.relu(_transformer_conv(x, src, dst, edge_attr, q1_w, q1_b, k1_w, k1_b, v1_w, v1_b, e1_w, s1_w, s1_b, n))
        h2 = jax.nn.relu(_transformer_conv(h1, src, dst, edge_attr, q2_w, q2_b, k2_w, k2_b, v2_w, v2_b, e2_w, s2_w, s2_b, n))
        skip_xs = jnp.concatenate([h1, h2], axis=-1)
        return jax.nn.relu(skip_xs @ skip_w + skip_b)

    def _L2_gnn_ref(h, weight, norm, src, dst, rel_type):
        import jax, jax.numpy as jnp
        import numpy as np
        N_NODES = 3125
        N_EDGES = 100000
        IN_FEAT = 64
        OUT_FEAT = 64
        NUM_RELS = 16
        n_nodes = h.shape[0]
        transformed = jnp.einsum('nd,rdo->nro', h, weight)
        msg = transformed[src, rel_type] * norm
        agg = jax.ops.segment_sum(msg, dst, num_segments=n_nodes)
        return jax.nn.relu(agg)

    def _L3_gnn_ref(x, edge_index, W1, b1, W2, b2):
        import jax, jax.numpy as jnp
        import numpy as np
        N_NODES = 50000
        N_EDGES = 25000
        FEAT = 64
        N_LAYERS = 3

        def _edgeconv(x, src, dst, W1, b1, W2, b2):
            xi = x[dst]
            xj = x[src]
            m = jnp.concatenate([xi, xj - xi], axis=-1)
            h = jax.nn.relu(m @ W1 + b1)
            h = h @ W2 + b2
            out = jax.ops.segment_max(h, dst, num_segments=x.shape[0])
            return jnp.where(jnp.isfinite(out), out, 0.0)
        src, dst = (edge_index[0], edge_index[1])
        for l in range(N_LAYERS):
            x = _edgeconv(x, src, dst, W1[l], b1[l], W2[l], b2[l])
            x = jax.nn.relu(x)
        return x
    edge_index = jnp.stack([src, dst])
    x = _layernorm(x + _L0_gnn_ref(x, edge_index), axis=-1)
    x = _layernorm(x + _L1_gnn_ref(x, edge_index, edge_attr_32, L1_gnn_q1_w, L1_gnn_q1_b, L1_gnn_k1_w, L1_gnn_k1_b, L1_gnn_v1_w, L1_gnn_v1_b, L1_gnn_e1_w, L1_gnn_s1_w, L1_gnn_s1_b, L1_gnn_q2_w, L1_gnn_q2_b, L1_gnn_k2_w, L1_gnn_k2_b, L1_gnn_v2_w, L1_gnn_v2_b, L1_gnn_e2_w, L1_gnn_s2_w, L1_gnn_s2_b, L1_gnn_skip_w, L1_gnn_skip_b), axis=-1)
    x = _layernorm(x + _L2_gnn_ref(x, L2_gnn_weight, edge_weight1, src, dst, edge_type_16), axis=-1)
    x = _layernorm(x + _L3_gnn_ref(x, edge_index, L3_gnn_W1, L3_gnn_b1, L3_gnn_W2, L3_gnn_b2), axis=-1)
    return x

_drawn_inputs = setup_inputs


def setup_inputs(seed=0):
    import zlib

    import numpy as np

    out = dict(_drawn_inputs(seed))
    spreads = {'L1_gnn_q1_b': (0.0, 0.292),
     'L1_gnn_k1_b': (0.0, 0.8),
     'L1_gnn_v1_b': (0.0, 0.1),
     'L1_gnn_s1_b': (0.0, 0.1),
     'L1_gnn_q2_b': (0.0, 0.506),
     'L1_gnn_k2_b': (0.0, 0.8),
     'L1_gnn_v2_b': (0.0, 0.1),
     'L1_gnn_s2_b': (0.0, 0.1),
     'L1_gnn_skip_b': (0.0, 0.1)}
    factors = {'L3_gnn_W1': 4.581, 'L3_gnn_b1': 4.916}
    for name, (base, spread) in spreads.items():
        noise = np.random.default_rng([zlib.crc32(name.encode()), seed]).standard_normal(out[name].shape)
        drawn = base * np.exp(spread * noise) if base else spread * noise
        out[name] = jnp.asarray(drawn.astype(out[name].dtype))
    for name, factor in factors.items():
        out[name] = (out[name] * factor).astype(out[name].dtype)
    return out
```

```python
from contextlib import ExitStack

import numpy as np

import concourse.bass as bass
from concourse import mybir

N, D, E, DE, R = 3125, 64, 103125, 32, 16
P = 128
TC = 4
EC = TC * P
C = -(-E // EC)
T = C * TC
EP = T * P
NB = -(-N // P)
NP = NB * P
NT = NP + P
GB = 4
GROUPS = [(b, min(GB, NB - b)) for b in range(0, NB, GB)]
G = len(GROUPS)
KA = D + DE + 1
U = 2
BIG = 1e38
EPS = 1e-5


def gnn_kernel(nc, src, typ, wgt, dst_row, dst_prev, dst_tile, first, edge_t, x, W, out):
    f32, i32, bf16, f8 = mybir.dt.float32, mybir.dt.int32, mybir.dt.bfloat16, mybir.dt.float8e4
    u8 = mybir.dt.uint8
    ALU, ACT, AX = mybir.AluOpType, mybir.ActivationFunctionType, mybir.AxisListType

    SUM, ATT, REL, MAX = "sum", "att", "rel", "max"
    ROUNDS = [SUM, ATT, ATT, REL, MAX, MAX, MAX]
    NR = len(ROUNDS)

    def dram(name, shape, dt):
        return nc.dram_tensor(name, shape, dt).ap()

    srcs = [dram(f"src_table{r}", (NP * R if k == REL else NP, D), f32) for r, k in enumerate(ROUNDS)]
    width = [{ATT: KA, MAX: D}.get(k, 0) for k in ROUNDS]
    dsts = [dram(f"dst_table{r}", (NT, 3 * w), bf16) if w else None for r, w in enumerate(width)]
    onehots = dram("onehots", (C, P, 2 * EC), u8)
    states = [dram("states_sum", (EP, D), f32), dram("states_att", (EP, KA), f32)]

    ctx = ExitStack()
    with ctx:
        def sb(name, shape, dt=f32):
            return ctx.enter_context(nc.sbuf_tensor(name, shape, dt))

        def sem(name):
            return ctx.enter_context(nc.semaphore(name))

        ps = ctx.enter_context(nc.psum_tensor("ps", [P, 8, EC], f32))

        ident = sb("ident", [P, P])
        shift = sb("shift", [P, 2, P])
        eighth = sb("eighth", [P, P])
        iota_i = sb("iota_i", [P, NB], i32)
        node_id = sb("node_id", [P, NB])
        eps = sb("eps", [P, 1])
        zrow = sb("zrow", [P, 3 * KA], bf16)
        wq = [sb(f"wq{l}", [D + 1, D]) for l in range(2)]
        wkeb = [sb(f"wkeb{l}", [KA, D]) for l in range(2)]
        wqT = [sb(f"wqT{l}", [D, D + 1]) for l in range(2)]
        wkebT = [sb(f"wkebT{l}", [D, KA]) for l in range(2)]
        wquery = [sb(f"wquery{l}", [D + 1, KA]) for l in range(2)]
        wvalue = [sb(f"wvalue{l}", [KA, D]) for l in range(2)]
        wself = [sb(f"wself{l}", [D + 1, D]) for l in range(2)]
        wskip1 = sb("wskip1", [D + 1, D])
        wskip2 = sb("wskip2", [D, D])
        wrel = sb("wrel", [D, R, D])
        w1 = sb("w1", [D, 3, 2 * D])
        w1a = sb("w1a", [D, 3, D])
        w2 = sb("w2", [D, 3, D])
        b1 = sb("b1", [D, 3])
        b2 = sb("b2", [P, 3, D])

        src_i = sb("src_i", [P, T], i32)
        rel_i = sb("rel_i", [P, T], i32)
        wgt_sb = sb("wgt_sb", [P, T])
        first_i = sb("first_i", [P, T], i32)
        first_f = sb("first_f", [P, T])
        base = sb("base", [P, T])
        mask = sb("mask", [P, T])
        tiles_le = sb("tiles_le", [P, NB])
        tile_i = sb("tile_i", [P, NB], i32)
        within = sb("within", [P, NB])
        edges_le = sb("edges_le", [P, NB + 1])
        last_f = sb("last_f", [P, NB])
        last_i = sb("last_i", [P, NB], i32)
        deg = sb("deg", [P, NB])
        dinv = sb("dinv", [P, NB])

        xn = sb("xn", [P, NB, D])
        zn = sb("zn", [P, NB, D])
        agg = sb("agg", [P, NB, P])
        dst_rows = agg[:, :, :].bitcast(i32)
        xT = sb("xT", [D + 1, NP])
        hT = sb("hT", [D + 1, NP])
        gy = sb("gy", [P, U, GB, D])
        gx = sb("gx", [P, U, GB, D])
        gs = sb("gs", [P, U, GB, D])
        ga = sb("ga", [P, U, 8, GB])
        rT = sb("rT", [KA, U, EC])
        split_r = sb("split_r", [P, U, GB * KA])
        split3 = sb("split3", [P, U, GB * 3 * KA], bf16)
        rel_rows = sb("rel_rows", [P, U, R * D])

        idx = sb("idx", [P, U, TC], i32)
        nodes = sb("nodes", [P, U, TC])
        rows = sb("rows", [P, U, TC, D])
        sel = sb("sel", [P, U, 2 * EC], f8)
        win = sb("win", [P, U, TC, 3 * KA], bf16)
        dst_b = sb("dst_b", [P, U, EC], i32)
        prev_b = sb("prev_b", [P, U, EC], i32)
        xe = sb("xe", [KA, U, EC])
        prod = sb("prod", [KA, U, EC])
        pen = sb("pen", [KA, U, EC])
        runmax = sb("runmax", [KA, 1 + U * EC])
        diff = sb("diff", [KA, U, EC])
        decay = sb("decay", [KA, U, EC])
        msg = sb("msg", [KA, U, EC])
        st = sb("st", [KA, U, EC])
        hb = sb("hb", [P, U, TC * KA])

        def bank(n, s):
            return ps[:, 2 * n + s, :]
        TURNED, QUERY, SCORE, BACK = range(4)

        loaded = sem("loaded")
        dve_pre = sem("dve_pre")
        act_pre = sem("act_pre")
        pe_pre = sem("pe_pre")
        pool_pre = sem("pool_pre")
        dst_rows_ready = sem("dst_rows_ready")
        zeros_stored = sem("zeros_stored")
        out_stored = sem("out_stored")
        rel_pe, rel_act = sem("rel_pe"), sem("rel_act")
        agg_ready = [sem(f"agg_ready{g}") for g in range(G)]

        LN = ["sum", "mean", "centred", "square", "var", "rstd", "norm"]
        SPLIT_D, SPLIT_A = ["rest", "low"], ["high", "middle"]
        STEPS = {
            0: (["scaled", "added"] + LN + SPLIT_D, ["std", "xT"] + SPLIT_A, ["turn_x", "query"]),
            1: (["inv", "alpha"] + SPLIT_D, ["rT", "relu", "hT"] + SPLIT_A, ["turn_r", "conv", "turn_h", "query"]),
            2: (["inv", "alpha", "added"] + LN, ["rT", "relu", "h2T", "skip", "std", "xT"],
                ["turn_r", "conv", "turn_h", "skip", "turn_x"]),
            3: (["added"] + LN + SPLIT_D, ["std", "xT", "src"] + SPLIT_A, ["turn_x", "pq"]),
            4: (["biased", "relu"] + SPLIT_D, ["zT", "src"] + SPLIT_A, ["turn_z", "pq"]),
            5: (["biased", "relu"] + SPLIT_D, ["zT", "src"] + SPLIT_A, ["turn_z", "pq"]),
            6: (["biased", "relu", "added"] + LN, ["std"], []),
        }

        class Signal:
            def __init__(self, sem_, before):
                self.sem, self.before = sem_, before

        kept = {}

        def shared(name, per_round):
            s_, before = kept.get(name) or (sem(name), 0)
            kept[name] = (s_, before + per_round)
            return Signal(s_, before)

        class Round:
            def __init__(self, r, kind):
                self.r, self.kind = r, kind
                self.idx_ready = shared("idx_ready", C)
                self.turned = shared("turned", C)
                self.st_ready = shared("st_ready", C)
                self.back = shared("back", C)
                self.hb_ready = shared("hb_ready", C)
                if kind == SUM:
                    self.sel_made = shared("sel_made", C)
                    self.nodes_ready = shared("nodes_ready", C)
                if kind == REL:
                    self.weighted = shared("weighted", C)
                if kind in (MAX, ATT):
                    self.pen_ready = shared("pen_ready", C)
                if kind == MAX:
                    self.relu_ready = shared("relu_ready", C)
                    self.lifted = shared("lifted", C)
                if kind == ATT:
                    self.xe_ready = shared("xe_ready", C)
                    self.query_ready = shared("query_ready", C)
                    self.prod_ready = shared("prod_ready", C)
                    self.score_ready = shared("score_ready", C)
                    self.carry_ready = shared("carry_ready", -(-C // U))
                    self.max_ready = shared("max_ready", C)
                    self.diff_ready = shared("diff_ready", C)
                    self.before_ready = shared("before_ready", C)
                    self.ddecay_ready = shared("ddecay_ready", C)
                    self.exp_ready = shared("exp_ready", C)
                    self.decay_ready = shared("decay_ready", C)
                    self.msg_ready = shared("msg_ready", C)
                self.rows_ready = [sem(f"rows_ready_{r}_{s_}") for s_ in range(U)]
                self.in_ready = [sem(f"in_ready_{r}_{s_}") for s_ in range(U)]
                uses = [(C - s_ + U - 1) // U for s_ in range(U)]
                self.st_stored = [shared(f"st_stored_{s_}", 16 * uses[s_]) for s_ in range(U)]
                if kind == ATT:
                    self.edge_ready = [shared(f"edge_ready_{s_}", 16 * uses[s_]) for s_ in range(U)]
                self.src_stored = [sem(f"src_stored_{r}_{s_}") for s_ in range(U if kind == REL else 1)]
                self.dst_stored = [sem(f"dst_stored_{r}_{s_}") for s_ in range(U if width[r] else 0)]
                self.dve, self.act, self.pe = (shared(f"node_{e}", G * len(STEPS[r][i]))
                                               for i, e in enumerate(("dve", "act", "pe")))

        rounds = [Round(r, k) for r, k in enumerate(ROUNDS)]
        N_LOADS = 3 + 3 + 1 + 2 * (2 + 3 + 3 + 2) + 3 + 1 + 3 + 2
        PRE_POOL = 13

        def wait(eng, *pairs):
            found = []
            for s, value in pairs:
                if isinstance(value, int) and value <= 0:
                    continue
                if isinstance(s, Signal):
                    s, value = s.sem, value + s.before
                found.append((s, value if isinstance(value, int) else eng.to_reg(value)))
            if not all(isinstance(value, int) for _, value in found):
                eng.wait_ge(pool_pre, PRE_POOL)
            for s, value in found:
                eng.wait_ge(s, value)

        def sources_stored(q):
            if q.kind == REL:
                return [(q.src_stored[s], 16 * ((NB - s + U - 1) // U)) for s in range(U)]
            return [(q.src_stored[0], 16 * (G if q.r else 1))]

        def tables_stored(q):
            return sources_stored(q) + [(x, 16 * ((G - s + U - 1) // U)) for s, x in enumerate(q.dst_stored)]

        def chunks(eng, lo, hi, body):
            while lo < min(U, hi):
                body(lo, lo % U, lo // U)
                lo += 1
            n = (hi - lo) // U
            if n > 0:
                with eng.Fori(0, n) as i:
                    for k in range(U):
                        body(U * i + (lo + k), (lo + k) % U, i + (lo + k) // U)
            for c in range(lo + max(n, 0) * U, hi):
                body(c, c % U, c // U)

        def cols(c, k=1):
            return slice(c * k, c * k + k) if isinstance(c, int) else bass.ds(c * k, k)

        def at(steps, g, name):
            return len(steps) * g + steps.index(name) + 1

        sel_stored = [sem(f"sel_stored{s}") for s in range(U)]
        N_LOADS = 6 + 2 * 10 + 3 + 1 + 5
        PRE_POOL = 13

        def part(i, u, nb, w):
            return split3[:, u, 0:nb * 3 * w].rearrange("p (b i f) -> p b i f", i=3, f=w)[:, :, i, :]

        def blocks_of(psum, nb, w):
            return psum[:, 0:nb * w].rearrange("p (b f) -> p b f", f=w)

        def split_act(act, q, sa, sd, sp_, g, nb, w, psum, made):
            u = g % U
            wait(act, (q.pe, made))
            if g >= U:
                act.wait_ge(rounds[q.r + 1].dst_stored[u], 16 * (g // U))
            nc.scalar.activation(part(0, u, nb, w), psum, ACT.Copy).then_inc(q.act.sem, 1)
            wait(act, (q.dve, at(sd, g, "rest")))
            nc.scalar.activation(part(1, u, nb, w),
                                 split_r[:, u, 0:nb * w].rearrange("p (b f) -> p b f", f=w),
                                 ACT.Copy).then_inc(q.act.sem, 1)

        def split_dve(dve, q, sa, sd, g, nb, w, psum):
            u = g % U
            left = split_r[:, u, 0:nb * w].rearrange("p (b f) -> p b f", f=w)
            wait(dve, (q.act, at(sa, g, "high")))
            nc.vector.tensor_tensor(left, psum, part(0, u, nb, w), ALU.subtract).then_inc(q.dve.sem, 1)
            wait(dve, (q.act, at(sa, g, "middle")), (q.dve, at(sd, g, "rest")))
            nc.vector.tensor_tensor(part(2, u, nb, w), left, part(1, u, nb, w),
                                    ALU.subtract).then_inc(q.dve.sem, 1)

        def node_stores(sp, q):
            r = q.r
            sd, sa, _ = STEPS[r]
            nxt = rounds[r + 1] if r + 1 < NR else None
            for g, (b, nb) in enumerate(GROUPS):
                rows_of = slice(b * P, (b + nb) * P)
                if r in (0, 1, 3, 4, 5):
                    if r == 0:
                        wait(sp, (q.dve, at(sd, g, "norm")))
                        data = xn
                    elif r == 1:
                        wait(sp, (q.act, at(sa, g, "relu")))
                        data = zn
                    else:
                        wait(sp, (q.act, at(sa, g, "src")))
                        data = zn
                    sp.dma_start(srcs[r + 1][rows_of, :].rearrange("(b p) f -> p b f", p=P),
                                 data[:, b:b + nb, :]).then_inc(nxt.src_stored[0], 16)
                    w = width[r + 1]
                    wait(sp, (q.dve, at(sd, g, "low")))
                    sp.dma_start(dsts[r + 1][rows_of, :].rearrange("(b p) f -> p b f", p=P),
                                 split3[:, g % U, 0:nb * 3 * w].rearrange("p (b f) -> p b f", f=3 * w))\
                        .then_inc(nxt.dst_stored[g % U], 16)
                if r == 6:
                    wait(sp, (q.dve, at(sd, g, "norm")))
                    real = min((b + nb) * P, N) - b * P
                    if real == nb * P:
                        sp.dma_start(out[rows_of, :].rearrange("(b p) f -> p b f", p=P),
                                     xn[:, b:b + nb, :]).then_inc(out_stored, 16)
                    else:
                        whole = real // P
                        if whole:
                            sp.dma_start(out[b * P:(b + whole) * P, :].rearrange("(b p) f -> p b f", p=P),
                                         xn[:, b:b + whole, :]).then_inc(out_stored, 16)
                        else:
                            sp.sem_inc(out_stored, 16)
                        sp.dma_start(out[(b + whole) * P:N, :], xn[0:N - (b + whole) * P, b + whole, :])\
                            .then_inc(out_stored, 16)
            if r == 2:
                for b in range(NB):
                    sp.wait_ge(rel_act, b + 1)
                    sp.dma_start(srcs[3][b * P * R:(b + 1) * P * R, :].rearrange("(p r) f -> p (r f)", p=P),
                                 rel_rows[:, b % U, :]).then_inc(nxt.src_stored[b % U], 16)

        def node_act(act, q):
            r = q.r
            sd, sa, sp_ = STEPS[r]
            for g, (b, nb) in enumerate(GROUPS):
                u, n = g % U, nb * P

                def turned(dst, name, rows_n):
                    wait(act, (q.pe, at(sp_, g, name)))
                    nc.scalar.activation(dst, bank(0, u)[0:rows_n, 0:n], ACT.Copy).then_inc(q.act.sem, 1)

                def std():
                    wait(act, (q.dve, at(sd, g, "var")))
                    nc.scalar.activation(ga[:, u, 3, 0:nb], ga[:, u, 2, 0:nb], ACT.Sqrt, bias=eps[:, :],
                                         scale=1.0 / D).then_inc(q.act.sem, 1)

                if r == 0:
                    std()
                    turned(xT[0:D, b * P:b * P + n], "turn_x", D)
                    split_act(act, q, sa, sd, sp_, g, nb, KA, blocks_of(bank(1, u), nb, KA), at(sp_, g, "query"))
                elif r == 1:
                    turned(rT[0:KA, u, 0:n], "turn_r", KA)
                    wait(act, (q.pe, at(sp_, g, "conv")))
                    nc.scalar.activation(zn[:, b:b + nb, :], blocks_of(bank(1, u), nb, D), ACT.Relu)\
                        .then_inc(q.act.sem, 1)
                    turned(hT[0:D, b * P:b * P + n], "turn_h", D)
                    split_act(act, q, sa, sd, sp_, g, nb, KA, blocks_of(bank(2, u), nb, KA), at(sp_, g, "query"))
                elif r == 2:
                    turned(rT[0:KA, u, 0:n], "turn_r", KA)
                    wait(act, (q.pe, at(sp_, g, "conv")))
                    nc.scalar.activation(gy[:, u, 0:nb, :], blocks_of(bank(1, u), nb, D), ACT.Relu)\
                        .then_inc(q.act.sem, 1)
                    turned(rT[0:D, u, 0:n], "turn_h", D)
                    wait(act, (q.pe, at(sp_, g, "skip")))
                    nc.scalar.activation(gs[:, u, 0:nb, :], blocks_of(bank(2, u), nb, D), ACT.Relu)\
                        .then_inc(q.act.sem, 1)
                    std()
                    turned(xT[0:D, b * P:b * P + n], "turn_x", D)
                elif r in (3, 4, 5):
                    if r == 3:
                        std()
                    turned((xT if r == 3 else hT)[0:D, b * P:b * P + n], "turn_x" if r == 3 else "turn_z", D)
                    wait(act, (q.pe, at(sp_, g, "pq")))
                    if r > 3:
                        pass
                    pq = blocks_of(bank(1, u), nb, 2 * D)
                    nc.scalar.activation(zn[:, b:b + nb, :], pq[:, :, D:2 * D], ACT.Copy).then_inc(q.act.sem, 1)
                    split_act(act, q, sa, sd, sp_, g, nb, D, pq[:, :, 0:D], at(sp_, g, "pq"))
                else:
                    std()
            if r == 2:
                for b in range(NB):
                    act.wait_ge(rel_pe, b + 1)
                    if b >= U:
                        act.wait_ge(rounds[3].src_stored[b % U], 16 * (b // U))
                    nc.scalar.activation(rel_rows[:, b % U, :].rearrange("p (a f) -> p a f", a=2),
                                         ps[:, 2 * (b % U):2 * (b % U) + 2, :], ACT.Copy).then_inc(rel_act, 1)

        def node_pe(pe, q):
            r = q.r
            sd, sa, sp_ = STEPS[r]
            for g, (b, nb) in enumerate(GROUPS):
                u, n = g % U, nb * P

                def turn(src_of, w, value, sem_):
                    wait(pe, (sem_, value))
                    for j in range(nb):
                        last = nc.tensor.matmul(bank(0, u)[0:w, j * P:(j + 1) * P], src_of(j), ident[:, :],
                                                is_transpose=True, start=True, stop=True)
                    last.then_inc(q.pe.sem, 1)

                def product(psum, w, terms):
                    for j in range(nb):
                        for i, (lhs, rhs) in enumerate(terms):
                            last = nc.tensor.matmul(psum[:, j * w:(j + 1) * w], lhs(j), rhs,
                                                    start=i == 0, stop=i == len(terms) - 1)
                    last.then_inc(q.pe.sem, 1)

                def of(m, rows_n):
                    return lambda j: m[0:rows_n, (b + j) * P:(b + j + 1) * P]

                def of_group(rows_n):
                    return lambda j: rT[0:rows_n, u, j * P:(j + 1) * P]

                free0 = {0: "xT", 1: "hT", 2: "xT", 3: "xT", 4: "zT", 5: "zT"}.get(r)
                if g >= U and free0:
                    wait(pe, (q.act, at(sa, g - U, free0)))
                if r == 0:
                    turn(lambda j: xn[:, b + j, :], D, at(sd, g, "norm"), q.dve)
                    wait(pe, (q.act, at(sa, g, "xT")))
                    if g >= U:
                        wait(pe, (q.dve, at(sd, g - U, "rest")))
                    product(bank(1, u), KA, [(of(xT, D + 1), wquery[0][:, :])])
                elif r in (1, 2):
                    turn(lambda j: agg[:, b + j, 0:KA], KA, at(sd, g, "alpha"), q.dve)
                    wait(pe, (q.act, at(sa, g, "rT")))
                    product(bank(1, u), D, [(of_group(KA), wvalue[r - 1][:, :]),
                                            (of(xT if r == 1 else hT, D + 1), wself[r - 1][:, :])])
                    if r == 1:
                        turn(lambda j: zn[:, b + j, :], D, at(sa, g, "relu"), q.act)
                        wait(pe, (q.act, at(sa, g, "hT")))
                        if g >= U:
                            wait(pe, (q.dve, at(sd, g - U, "rest")))
                        product(bank(2, u), KA, [(of(hT, D + 1), wquery[1][:, :])])
                    else:
                        turn(lambda j: gy[:, u, j, :], D, at(sa, g, "relu"), q.act)
                        wait(pe, (q.act, at(sa, g, "h2T")))
                        product(bank(2, u), D, [(of(hT, D + 1), wskip1[:, :]), (of_group(D), wskip2[:, :])])
                        turn(lambda j: xn[:, b + j, :], D, at(sd, g, "norm"), q.dve)
                elif r in (3, 4, 5):
                    if r == 3:
                        turn(lambda j: xn[:, b + j, :], D, at(sd, g, "norm"), q.dve)
                    else:
                        turn(lambda j: zn[:, b + j, :], D, at(sd, g, "relu"), q.dve)
                    wait(pe, (q.act, at(sa, g, "xT" if r == 3 else "zT")))
                    if g >= U:
                        wait(pe, (q.dve, at(sd, g - U, "rest")), (q.act, at(sa, g - U, "high")))
                    product(bank(1, u), 2 * D, [(of(xT if r == 3 else hT, D), w1[:, r - 3, :])])
            if r == 2:
                wait(pe, (q.act, at(sa, G - 1, "xT")))
                for b in range(NB):
                    if b >= U:
                        pe.wait_ge(rel_act, b - U + 1)
                    for i in range(2):
                        last = nc.tensor.matmul(ps[:, 2 * (b % U) + i, :], xT[0:D, b * P:(b + 1) * P],
                                                wrel[:, i * R // 2:(i + 1) * R // 2, :].rearrange("d r o -> d (r o)"),
                                                start=True, stop=True)
                    last.then_inc(rel_pe, 1)

        def node_dve(dve, q):
            r = q.r
            sd, sa, sp_ = STEPS[r]
            for g, (b, nb) in enumerate(GROUPS):
                u = g % U
                y, xc, sq = gy[:, u, 0:nb, :], gx[:, u, 0:nb, :], gs[:, u, 0:nb, :]
                x_g, z_g, a_g = xn[:, b:b + nb, :], zn[:, b:b + nb, :], agg[:, b:b + nb, 0:D]
                small = lambda i: ga[:, u, i, 0:nb]
                wide = lambda v, w: v.unsqueeze(2).to_broadcast([P, nb, w])

                def op(name, ins):
                    ins.then_inc(q.dve.sem, 1)
                    wait(dve, (q.dve, at(sd, g, name)))

                def layer_norm(v):
                    op("sum", nc.vector.reduce_sum(small(0), v, axis=AX.X))
                    op("mean", nc.vector.tensor_scalar(small(1), small(0), -1.0 / D, None, ALU.mult))
                    op("centred", nc.vector.tensor_tensor(xc, v, wide(small(1), D), ALU.add))
                    op("square", nc.vector.tensor_tensor(sq, xc, xc, ALU.mult))
                    op("var", nc.vector.reduce_sum(small(2), sq, axis=AX.X))
                    wait(dve, (q.act, at(sa, g, "std")))
                    op("rstd", nc.vector.reciprocal(small(4), small(3)))
                    op("norm", nc.vector.tensor_tensor(x_g, xc, wide(small(4), D), ALU.mult))

                dve.wait_ge(agg_ready[g], 16 * nb * (r + 1))
                if r == 0:
                    op("scaled", nc.vector.tensor_tensor(y, a_g, wide(dinv[:, b:b + nb], D), ALU.mult))
                    op("added", nc.vector.tensor_tensor(y, y, x_g, ALU.add))
                    layer_norm(y)
                    split_dve(dve, q, sa, sd, g, nb, KA, blocks_of(bank(1, u), nb, KA))
                elif r in (1, 2):
                    a_k = agg[:, b:b + nb, 0:KA]
                    op("inv", nc.vector.reciprocal(small(0).unsqueeze(2), agg[:, b:b + nb, KA - 1:KA]))
                    op("alpha", nc.vector.tensor_tensor(a_k, a_k, wide(small(0), KA), ALU.mult))
                    if r == 1:
                        split_dve(dve, q, sa, sd, g, nb, KA, blocks_of(bank(2, u), nb, KA))
                    else:
                        wait(dve, (q.act, at(sa, g, "skip")))
                        op("added", nc.vector.tensor_tensor(y, sq, x_g, ALU.add))
                        layer_norm(y)
                elif r == 3:
                    op("added", nc.vector.scalar_tensor_tensor(y, a_g, 0.0, x_g, ALU.max, ALU.add))
                    layer_norm(y)
                    split_dve(dve, q, sa, sd, g, nb, D, blocks_of(bank(1, u), nb, 2 * D)[:, :, 0:D])
                else:
                    b2_l = b2[:, r - 4, :].unsqueeze(1).to_broadcast([P, nb, D])
                    op("biased", nc.vector.tensor_tensor(y, a_g, b2_l, ALU.add))
                    op("relu", nc.vector.tensor_scalar(z_g, y, 0.0, None, ALU.max))
                    if r < 6:
                        split_dve(dve, q, sa, sd, g, nb, D, blocks_of(bank(1, u), nb, 2 * D)[:, :, 0:D])
                    else:
                        op("added", nc.vector.tensor_tensor(y, z_g, x_g, ALU.add))
                        layer_norm(y)

        block = ctx.enter_context(nc.Block())

        @block.sync
        def _(sp):
            def load(dst, s):
                sp.dma_start(dst, s).then_inc(loaded, 16)

            load(first_i[:, :], first.to_broadcast([P, T]))
            load(src_i[:, :], src)
            load(rel_i[:, :], typ)
            load(wgt_sb[:, :], wgt)
            full = N // P
            load(xn[:, 0:full, :], x[0:full * P, :].rearrange("(b p) f -> p b f", p=P))
            for l in range(2):
                n = l + 1
                row = lambda name: W[name].rearrange("(a n) -> a n", a=1)
                load(wq[l][0:D, :], W[f"q{n}_w"])
                load(wq[l][D:D + 1, :], row(f"q{n}_b"))
                load(wkeb[l][0:D, :], W[f"k{n}_w"])
                load(wkeb[l][D:D + DE, :], W[f"e{n}_w"])
                load(wkeb[l][KA - 1:KA, :], row(f"k{n}_b"))
                load(wvalue[l][0:D, :], W[f"v{n}_w"])
                load(wvalue[l][D:D + DE, :], W[f"e{n}_w"])
                load(wvalue[l][KA - 1:KA, :], row(f"v{n}_b"))
                load(wself[l][0:D, :], W[f"s{n}_w"])
                load(wself[l][D:D + 1, :], row(f"s{n}_b"))
            load(wskip1[0:D, :], W["skip_w"][0:D, :])
            load(wskip1[D:D + 1, :], W["skip_b"].rearrange("(a n) -> a n", a=1))
            load(wskip2[:, :], W["skip_w"][D:2 * D, :])
            load(wrel[:, :, :], W["rel"].rearrange("r d o -> d r o"))
            load(w1a[:, :, :], W["W1"][:, 0:D, :].rearrange("l d o -> d l o"))
            load(w1[:, :, D:2 * D], W["W1"][:, D:2 * D, :].rearrange("l d o -> d l o"))
            load(w2[:, :, :], W["W2"].rearrange("l d o -> d l o"))
            load(b1[:, :], W["b1"])
            load(b2[:, :, :].rearrange("p l o -> p (l o)"),
                 W["b2"].rearrange("(a l) o -> a (l o)", a=1).to_broadcast([P, 3 * D]))
            sp.wait_ge(pool_pre, PRE_POOL)
            load(xn[0:N - full * P, full, :], x[full * P:N, :])
            for r in range(NR):
                if width[r]:
                    sp.dma_start(dsts[r][NP:NT, :], zrow[:, 0:3 * width[r]]).then_inc(zeros_stored, 16)
            sp.wait_ge(dve_pre, PRE_SCALED)
            sp.dma_start(srcs[0].rearrange("(b p) f -> p b f", p=P), zn[:, :, :]).then_inc(rounds[0].src_stored[0], 16)

            for q in rounds:
                r, k = q.r, q.kind
                kw = KA if k == ATT else D
                table = states[1] if k == ATT else states[0]

                def store_states(c, s, n):
                    wait(sp, (q.hb_ready, c + 1))
                    e = slice(c * EC, (c + 1) * EC) if isinstance(c, int) else bass.ds(c * EC, EC)
                    sp.dma_start(table[e, :].rearrange("(j p) f -> p j f", p=P),
                                 hb[:, s, 0:TC * kw].rearrange("p (j f) -> p j f", f=kw))\
                        .then_inc(q.st_stored[s].sem, 16)

                def one(c):
                    return c if isinstance(c, int) else bass.ds(c, 1)

                def fetch(c, s, n):
                    e = slice(c * EC, (c + 1) * EC) if isinstance(c, int) else bass.ds(c * EC, EC)
                    if k == SUM:
                        wait(sp, (q.sel_made, c - U + 1))
                        sp.dma_start(dst_b[:, s, :], dst_row[:, e].to_broadcast([P, EC])).then_inc(q.in_ready[s], 16)
                        sp.dma_start(prev_b[:, s, :], dst_prev[:, e].to_broadcast([P, EC])).then_inc(q.in_ready[s], 16)
                        return
                    used = [q.st_ready] if k == REL else [q.pen_ready, q.query_ready if k == ATT else q.turned]
                    wait(sp, *[(u, c - U + 1) for u in used])
                    o = onehots[one(c)]
                    o = o if isinstance(c, int) else o.rearrange("a p e -> (a p) e")
                    if k == REL:
                        sp.dma_start(sel[:, s, EC:].bitcast(u8), o[:, EC:]).then_inc(q.in_ready[s], 16)
                        return
                    sp.dma_start(sel[:, s, :].bitcast(u8), o).then_inc(q.in_ready[s], 16)
                    for j in range(TC):
                        t = c * TC + j
                        v = sp.value_load(first_i[0:1, slice(t, t + 1) if isinstance(c, int) else bass.ds(t, 1)],
                                          min_val=0, max_val=NP)
                        sp.dma_start(win[:, s, j, 0:3 * kw], dsts[r][bass.ds(v, P), :]).then_inc(q.in_ready[s], 16)
                    if k == ATT:
                        wait(sp, (q.msg_ready, c - U + 1))
                        sp.dma_start(xe[D:D + DE, s, :], edge_t[:, e]).then_inc(q.edge_ready[s].sem, 16)

                def step(c, s, n):
                    fetch(c, s, n)
                    if not isinstance(c, int) or c >= U:
                        store_states(c - U, s, n - 1)
                    if k == SUM:
                        store_onehots(c, s, n)

                def store_onehots(c, s, n):
                    wait(sp, (q.sel_made, c + 1))
                    o = onehots[one(c)]
                    o = o if isinstance(c, int) else o.rearrange("a p e -> (a p) e")
                    sp.dma_start(o, sel[:, s, :].bitcast(u8)).then_inc(sel_stored[s], 16)

                if r == 0:
                    pass
                else:
                    if r == 1:
                        for s in range(U):
                            sp.wait_ge(sel_stored[s], 16 * ((C - s + U - 1) // U))
                        sp.wait_ge(zeros_stored, 16 * sum(w > 0 for w in width))
                    wait(sp, *tables_stored(q))
                chunks(sp, 0, C, step)
                for c in range(C - U, C):
                    store_states(c, c % U, c // U)
                node_stores(sp, q)
            sp.wait_ge(out_stored, 16 * (G + 1))

        @block.gpsimd
        def _(pool):
            pool.memset(ident[:, :], 0.0).then_inc(pool_pre, 1)
            pool.memset(shift[:, :, :], 0.0).then_inc(pool_pre, 1)
            pool.memset(eighth[:, :], float(D) ** -0.5).then_inc(pool_pre, 1)
            pool.memset(zrow[:, :], 0.0).then_inc(pool_pre, 1)
            pool.memset(eps[:, :], EPS).then_inc(pool_pre, 1)
            pool.memset(xT[:, :], 1.0).then_inc(pool_pre, 1)
            pool.memset(hT[:, :], 1.0).then_inc(pool_pre, 1)
            pool.memset(xe[:, :, :], 1.0).then_inc(pool_pre, 1)
            pool.memset(xn[:, NB - 1, :], 0.0).then_inc(pool_pre, 1)
            nc.gpsimd.iota(iota_i[:, :], pattern=[[P, NB]], base=0, channel_multiplier=1).then_inc(pool_pre, 1)
            pool.wait_ge(pool_pre, 2)
            nc.gpsimd.affine_select(out=ident[:, :], in_=ident[:, :], compare_op=ALU.not_equal, fill=1.0,
                                    base=0, pattern=[[-1, P]], channel_multiplier=1).then_inc(pool_pre, 1)
            nc.gpsimd.affine_select(out=shift[:, 0, :], in_=shift[:, 0, :], compare_op=ALU.not_equal, fill=1.0,
                                    base=1, pattern=[[-1, P]], channel_multiplier=1).then_inc(pool_pre, 1)
            nc.gpsimd.affine_select(out=shift[:, 1, :], in_=shift[:, 1, :], compare_op=ALU.not_equal, fill=1.0,
                                    base=-(P - 1), pattern=[[-1, P]], channel_multiplier=1).then_inc(pool_pre, 1)

            pool.wait_ge(dve_pre, PRE_TILES)
            for b in range(NB):
                pool.indirect_dma_start(dst_rows[:, b, :], None, dst_tile,
                                        bass.IndirectOffsetOnAxis(ap=tile_i[:, b:b + 1], axis=0))\
                    .then_inc(dst_rows_ready, 16)

            for q in rounds:
                def gather(c, s, n):
                    wait(pool, *sources_stored(q), (q.idx_ready, c + 1), (q.turned, c - U + 1))
                    for j in range(TC):
                        pool.indirect_dma_start(rows[:, s, j, :], None, srcs[q.r],
                                                bass.IndirectOffsetOnAxis(ap=idx[:, s, j:j + 1], axis=0))\
                            .then_inc(q.rows_ready[s], 16)
                chunks(pool, 0, C, gather)
                kw = KA if q.kind == ATT else D
                for s in range(U):
                    wait(pool, (q.st_stored[s], 16 * ((C - s + U - 1) // U)))
                for g, (b0, nb) in enumerate(GROUPS):
                    for b in range(b0, b0 + nb):
                        pool.indirect_dma_start(agg[:, b, 0:kw], None, states[1] if q.kind == ATT else states[0],
                                                bass.IndirectOffsetOnAxis(ap=last_i[:, b:b + 1], axis=0))\
                            .then_inc(agg_ready[g], 16)

        @block.scalar
        def _(act):
            act.wait_ge(pool_pre, PRE_POOL)
            for l in range(2):
                act.wait_ge(pe_pre, 2 * l + 2)
                nc.scalar.activation(wqT[l][:, :], bank(0, l)[0:D, 0:D + 1], ACT.Copy).then_inc(act_pre, 1)
                nc.scalar.activation(wkebT[l][:, :], bank(0, l)[0:D, P:P + KA], ACT.Copy).then_inc(act_pre, 1)
            act.wait_ge(pe_pre, 6)
            for l in range(2):
                nc.scalar.activation(wquery[l][:, :], bank(1, l)[0:D + 1, 0:KA], ACT.Copy).then_inc(act_pre, 1)
            act.wait_ge(dve_pre, PRE_DEG)
            nc.scalar.activation(deg[:, :], deg[:, :], ACT.Sqrt).then_inc(act_pre, 1)

            for q in rounds:
                k = q.kind
                kw = KA if k == ATT else D

                def indices(c, s, n):
                    if k == SUM:
                        wait(act, (q.sel_made, c - U + 1))
                        nc.scalar.activation(nodes[:, s, :], base[:, cols(c, TC)], ACT.Copy).then_inc(q.nodes_ready.sem, 1)
                    wait(act, (q.rows_ready[s], 64 * n))
                    src_idx = rel_i if k == REL else src_i
                    nc.scalar.activation(idx[:, s, :], src_idx[:, cols(c, TC)], ACT.Copy).then_inc(q.idx_ready.sem, 1)

                def penalty(c, s, n):
                    wait(act, (q.in_ready[s], 16 * (TC + 1) * (n + 1)),
                         (q.before_ready if k == ATT else q.st_ready, c - U + 1))
                    nc.scalar.activation(pen[0:kw, s, :], sel[0:kw, s, EC:], ACT.Copy, scale=BIG, bias=-BIG)\
                        .then_inc(q.pen_ready.sem, 1)

                def states_out(c, s, n):
                    wait(act, (q.back, c + 1), (q.st_stored[s], 16 * n))
                    nc.scalar.activation(hb[:, s, 0:TC * kw], bank(BACK, s)[:, 0:TC * kw], ACT.Copy)\
                        .then_inc(q.hb_ready.sem, 1)

                def exponentials(c, s, n):
                    wait(act, (q.diff_ready, c + 1))
                    nc.scalar.activation(diff[:, s, :], diff[:, s, :], ACT.Exp).then_inc(q.exp_ready.sem, 1)
                    wait(act, (q.ddecay_ready, c + 1))
                    nc.scalar.activation(decay[:, s, :], decay[:, s, :], ACT.Exp).then_inc(q.decay_ready.sem, 1)

                def step(c, s, n):
                    later = not isinstance(c, int)
                    if k == ATT:
                        wait(act, (q.turned, c + 1), (q.msg_ready, c - U + 1))
                        nc.scalar.activation(xe[0:D, s, :], bank(TURNED, s)[0:D, :], ACT.Copy)\
                            .then_inc(q.xe_ready.sem, 1)
                    if k == MAX:
                        wait(act, (q.turned, c + 1), (q.lifted, c - U + 1))
                        nc.scalar.activation(xe[0:D, s, :], bank(TURNED, s)[0:D, :], ACT.Relu,
                                             bias=b1[:, q.r - 4:q.r - 3]).then_inc(q.relu_ready.sem, 1)
                    if later or c + U < C:
                        indices(c + U, s, n + 1)
                    if k in (ATT, MAX):
                        penalty(c, s, n)
                    if k == ATT:
                        if later or c >= 1:
                            exponentials(c - 1, (s - 1) % U, None)
                        if later or c >= 2:
                            states_out(c - 2, s, n - 1)
                    elif later or c >= 1:
                        states_out(c - 1, (s - 1) % U, n - (1 if s == 0 else 0))

                for c in range(U):
                    indices(c, c, 0)
                chunks(act, 0, C - U, step)
                for c in range(C - U, C):
                    step(c, c % U, c // U)
                if k == ATT:
                    exponentials(C - 1, (C - 1) % U, None)
                    states_out(C - 2, (C - 2) % U, (C - 2) // U)
                states_out(C - 1, (C - 1) % U, (C - 1) // U)
                node_act(act, q)

        @block.tensor
        def _(pe):
            pe.wait_ge(pool_pre, PRE_POOL)
            pe.wait_ge(loaded, 16 * N_LOADS)
            for l in range(2):
                nc.tensor.transpose(bank(0, l)[0:D, 0:D + 1], wq[l][:, :], ident[0:D + 1, 0:D + 1]).then_inc(pe_pre, 1)
                nc.tensor.transpose(bank(0, l)[0:D, P:P + KA], wkeb[l][:, :], ident[0:KA, 0:KA]).then_inc(pe_pre, 1)
            pe.wait_ge(act_pre, 4)
            for l in range(2):
                nc.tensor.matmul(bank(1, l)[0:D + 1, 0:KA], wqT[l][:, :], wkebT[l][:, :], start=True, stop=True)\
                    .then_inc(pe_pre, 1)
            pe.wait_ge(dve_pre, PRE_EDGES)
            nc.tensor.matmul(bank(2, 0)[:, 0:NB], shift[:, 0, :], edges_le[:, 1:NB + 1], start=True, stop=False)
            nc.tensor.matmul(bank(2, 0)[:, 0:NB], shift[:, 1, :], edges_le[:, 0:NB], start=False, stop=True)\
                .then_inc(pe_pre, 1)

            for q in rounds:
                k = q.kind
                kw = KA if k == ATT else D

                def turn(c, s, n):
                    made = {REL: [(q.weighted, c + 1)] if k == REL else [],
                            MAX: [(q.in_ready[s], 16 * (TC + 1) * (n + 1))]}.get(k, [])
                    emptied = q.xe_ready if k == ATT else q.relu_ready if k == MAX else q.st_ready
                    wait(pe, (q.rows_ready[s], 64 * (n + 1)), *made, (emptied, c - U + 1))
                    for j in range(TC):
                        o = bank(TURNED, s)[0:D, j * P:(j + 1) * P]
                        last = nc.tensor.matmul(o, rows[:, s, j, :], ident[:, :], is_transpose=True,
                                                start=True, stop=k != MAX)
                        if k == MAX:
                            for i in range(3):
                                last = nc.tensor.matmul(o, win[:, s, j, i * kw:(i + 1) * kw],
                                                        sel[:, s, j * P:(j + 1) * P], start=False, stop=i == 2)
                    last.then_inc(q.turned.sem, 1)

                def query(c, s, n):
                    wait(pe, (q.in_ready[s], 16 * (TC + 1) * (n + 1)), (q.prod_ready, c - U + 1))
                    for j in range(TC):
                        for i in range(3):
                            last = nc.tensor.matmul(bank(QUERY, s)[0:KA, j * P:(j + 1) * P],
                                                    win[:, s, j, i * KA:(i + 1) * KA],
                                                    sel[:, s, j * P:(j + 1) * P], start=i == 0, stop=i == 2)
                    last.then_inc(q.query_ready.sem, 1)

                def score(c, s, n):
                    wait(pe, (q.prod_ready, c + 1), (q.diff_ready, c - U + 1))
                    nc.tensor.matmul(bank(SCORE, s)[0:KA, :], eighth[0:KA, 0:KA], prod[:, s, :],
                                     start=True, stop=True).then_inc(q.score_ready.sem, 1)

                def lift(c, s, n):
                    wait(pe, (q.relu_ready, c + 1), (q.st_ready, c - U + 1))
                    nc.tensor.matmul(bank(QUERY, s)[0:D, :], w2[:, q.r - 4, :], xe[0:D, s, :],
                                     start=True, stop=True).then_inc(q.lifted.sem, 1)

                def back(c, s, n):
                    wait(pe, (q.st_ready, c + 1), (q.hb_ready, c - U + 1))
                    for j in range(TC):
                        last = nc.tensor.matmul(bank(BACK, s)[:, j * kw:(j + 1) * kw],
                                                st[0:kw, s, j * P:(j + 1) * P], ident[0:kw, 0:kw],
                                                is_transpose=True, start=True, stop=True)
                    last.then_inc(q.back.sem, 1)

                def step(c, s, n):
                    turn(c, s, n)
                    if k == ATT:
                        query(c, s, n)
                        score(c, s, n)
                    if k == MAX:
                        lift(c, s, n)
                    if not isinstance(c, int) or c >= 1:
                        back(c - 1, (s - 1) % U, None)

                chunks(pe, 0, C, step)
                back(C - 1, (C - 1) % U, None)
                node_pe(pe, q)

        @block.vector
        def _(dve):
            made = [0]

            def pre(ins):
                made[0] += 1
                ins.then_inc(dve_pre, 1)
                dve.wait_ge(dve_pre, made[0])

            dve.wait_ge(pool_pre, PRE_POOL)
            dve.wait_ge(loaded, 16 * N_LOADS)
            pre(nc.vector.tensor_copy(node_id[:, :], iota_i[:, :]))
            pre(nc.vector.tensor_copy(first_f[:, :], first_i[:, :]))
            pre(nc.vector.tensor_scalar(base[:, :], first_f[:, :], node_id[:, 0:1], None, ALU.add))
            for b in range(NB):
                pre(nc.vector.tensor_scalar(mask[:, :], first_f[:, :], node_id[:, b:b + 1], None, ALU.is_le))
                pre(nc.vector.reduce_sum(tiles_le[:, b:b + 1], mask[:, :], axis=AX.X))
            pre(nc.vector.tensor_scalar(tiles_le[:, :], tiles_le[:, :], -1.0, 0.0, ALU.add, ALU.max))
            pre(nc.vector.tensor_copy(tile_i[:, :], tiles_le[:, :]))
            assert made[0] == PRE_TILES
            pre(nc.vector.memset(edges_le[:, 0:1], 0.0))
            pre(nc.vector.tensor_scalar(mask[:, :], src_i[:, :], float(R), None, ALU.mult))
            pre(nc.vector.tensor_tensor(mask[:, :], mask[:, :], rel_i[:, :], ALU.add))
            pre(nc.vector.tensor_copy(rel_i[:, :], mask[:, :]))
            pre(nc.vector.tensor_tensor(w1[:, :, 0:D], w1a[:, :, :], w1[:, :, D:2 * D], ALU.subtract))
            dve.wait_ge(dst_rows_ready, 16 * NB)
            pre(nc.vector.tensor_tensor(agg[:, :, :], dst_rows, node_id[:, :].unsqueeze(2).to_broadcast([P, NB, P]),
                                        ALU.is_le))
            pre(nc.vector.reduce_sum(within[:, :], agg[:, :, :], axis=AX.X))
            pre(nc.vector.scalar_tensor_tensor(edges_le[:, 1:NB + 1], tiles_le[:, :], float(P), within[:, :],
                                               ALU.mult, ALU.add))
            assert made[0] == PRE_EDGES
            pre(nc.vector.tensor_scalar(last_f[:, :], edges_le[:, 1:NB + 1], -1.0, 0.0, ALU.add, ALU.max))
            pre(nc.vector.tensor_copy(last_i[:, :], last_f[:, :]))
            dve.wait_ge(pe_pre, 7)
            pre(nc.vector.tensor_tensor(deg[:, :], edges_le[:, 1:NB + 1], bank(2, 0)[:, 0:NB], ALU.subtract))
            pre(nc.vector.tensor_scalar(deg[:, :], deg[:, :], 1.0, None, ALU.max))
            assert made[0] == PRE_DEG
            dve.wait_ge(act_pre, 7)
            pre(nc.vector.reciprocal(dinv[:, :], deg[:, :]))
            pre(nc.vector.tensor_tensor(zn[:, :, :], xn[:, :, :], dinv[:, :].unsqueeze(2).to_broadcast([P, NB, D]),
                                        ALU.mult))
            assert made[0] == PRE_SCALED

            for q in rounds:
                k = q.kind
                kw = KA if k == ATT else D

                def scan(c, s, d0, d1, op0, op1):
                    wait(dve, (q.back, c - U + 1), (q.st_ready, c))
                    first_one = isinstance(c, int) and c == 0
                    init = (0.0 if op1 == ALU.add else -BIG) if first_one else st[0:kw, (s - 1) % U, EC - 1:EC]
                    nc.vector.tensor_tensor_scan(st[0:kw, s, :], d0, d1, init, op0, op1).then_inc(q.st_ready.sem, 1)

                def make_onehots(c, s, n):
                    wait(dve, (q.in_ready[s], 32 * (n + 1)), (q.nodes_ready, c + 1), (sel_stored[s], 16 * n))
                    nc.vector.tensor_tensor(sel[:, s, EC:], dst_b[:, s, :], prev_b[:, s, :], ALU.is_equal,
                                            saturate=False)
                    for j in range(TC):
                        last = nc.vector.tensor_scalar(sel[:, s, j * P:(j + 1) * P], dst_b[:, s, j * P:(j + 1) * P],
                                                       nodes[:, s, j:j + 1], None, ALU.is_equal, saturate=False)
                    last.then_inc(q.sel_made.sem, 1)

                def step_plain(c, s, n):
                    if k == SUM:
                        make_onehots(c, s, n)
                        wait(dve, (q.sel_made, c + 1))
                    if k == REL:
                        wait(dve, (q.rows_ready[s], 64 * (n + 1)))
                        nc.vector.tensor_tensor(rows[:, s, :, :], rows[:, s, :, :],
                                                wgt_sb[:, cols(c, TC)].unsqueeze(2).to_broadcast([P, TC, D]),
                                                ALU.mult).then_inc(q.weighted.sem, 1)
                        wait(dve, (q.in_ready[s], 16 * (n + 1)))
                    if k == MAX:
                        wait(dve, (q.lifted, c + 1), (q.pen_ready, c + 1))
                        scan(c, s, pen[0:D, s, :], bank(QUERY, s)[0:D, :], ALU.add, ALU.max)
                    else:
                        wait(dve, (q.turned, c + 1))
                        scan(c, s, sel[0:D, s, EC:], bank(TURNED, s)[0:D, :], ALU.mult, ALU.add)

                def product(c, s, n):
                    wait(dve, (q.query_ready, c + 1),
                         (q.xe_ready, c + 1),
                         (q.edge_ready[s], 16 * (n + 1)),
                         (q.score_ready, c - U + 1))
                    nc.vector.tensor_tensor(prod[:, s, :], bank(QUERY, s)[0:KA, :], xe[:, s, :], ALU.mult)\
                        .then_inc(q.prod_ready.sem, 1)

                def accumulate(c, s, n):
                    wait(dve, (q.exp_ready, c + 1), (q.xe_ready, c + 1))
                    nc.vector.tensor_tensor(msg[:, s, :], diff[:, s, :], xe[:, s, :], ALU.mult)\
                        .then_inc(q.msg_ready.sem, 1)
                    wait(dve, (q.decay_ready, c + 1), (q.msg_ready, c + 1))
                    scan(c, s, decay[:, s, :], msg[:, s, :], ALU.mult, ALU.add)

                def maxima(c, s, n):
                    m = runmax[:, 1 + s * EC:1 + (s + 1) * EC]
                    before = runmax[:, s * EC:(s + 1) * EC]
                    if isinstance(c, int) and c == 0:
                        nc.vector.memset(runmax[:, 0:1], -BIG).then_inc(q.carry_ready.sem, 1)
                        wait(dve, (q.carry_ready, 1))
                    elif s == 0:
                        wait(dve, (q.max_ready, c))
                        nc.vector.tensor_copy(runmax[:, 0:1], runmax[:, U * EC:U * EC + 1]).then_inc(q.carry_ready.sem, 1)
                        wait(dve, (q.carry_ready, n + 1))
                    wait(dve, (q.max_ready, c), (q.score_ready, c + 1), (q.pen_ready, c + 1))
                    nc.vector.tensor_tensor_scan(m, pen[:, s, :], bank(SCORE, s)[0:KA, :], before[:, 0:1],
                                                 ALU.add, ALU.max).then_inc(q.max_ready.sem, 1)
                    wait(dve, (q.max_ready, c + 1), (q.msg_ready, c - U + 1))
                    nc.vector.tensor_tensor(diff[:, s, :], bank(SCORE, s)[0:KA, :], m, ALU.subtract)\
                        .then_inc(q.diff_ready.sem, 1)
                    wait(dve, (q.st_ready, c - U + 1))
                    nc.vector.tensor_tensor(decay[:, s, :], before, pen[:, s, :], ALU.add).then_inc(q.before_ready.sem, 1)
                    wait(dve, (q.before_ready, c + 1))
                    nc.vector.tensor_tensor(decay[:, s, :], decay[:, s, :], m, ALU.subtract)\
                        .then_inc(q.ddecay_ready.sem, 1)

                def step_att(c, s, n):
                    product(c, s, n)
                    if not isinstance(c, int) or c >= 1:
                        accumulate(c - 1, (s - 1) % U, None)
                    maxima(c, s, n)

                chunks(dve, 0, C, step_att if k == ATT else step_plain)
                if k == ATT:
                    accumulate(C - 1, (C - 1) % U, None)
                node_dve(dve, q)

_WEIGHTS = ["q1_w", "q1_b", "k1_w", "k1_b", "v1_w", "v1_b", "e1_w", "s1_w", "s1_b", "q2_w", "q2_b", "k2_w",
            "k2_b", "v2_w", "v2_b", "e2_w", "s2_w", "s2_b", "skip_w", "skip_b"]

PRE_TILES = 3 + 2 * NB + 2
PRE_EDGES = PRE_TILES + 5 + 3
PRE_DEG = PRE_EDGES + 4
PRE_SCALED = PRE_DEG + 2


def kernel(**inputs):
    import concourse.bacc as _bacc
    from concourse.bass_utils import run_bass_kernel_spmd as _run

    def padded(a, value):
        a = np.asarray(a).reshape(-1)
        return np.concatenate([a, np.full(EP - E, value, a.dtype)])

    def tiled(a, value):
        return np.ascontiguousarray(padded(a, value).reshape(T, P).T)

    dst = padded(inputs["dst"], N)
    edge = np.asarray(inputs["edge_attr_32"])
    arrays = {
        "src": tiled(inputs["src"], 0),
        "typ": tiled(inputs["edge_type_16"], 0),
        "wgt": tiled(inputs["edge_weight1"], 0),
        "dst_row": dst.reshape(1, EP),
        "dst_prev": np.concatenate([np.full(1, -1, dst.dtype), dst[:-1]]).reshape(1, EP),
        "dst_tile": dst.reshape(T, P),
        "first": np.ascontiguousarray(dst[::P]).reshape(1, T),
        "edge_t": np.ascontiguousarray(np.concatenate([edge, np.zeros((EP - E, DE), edge.dtype)]).T),
        "x": np.ascontiguousarray(inputs["x"]),
    }
    for w in _WEIGHTS:
        arrays[w] = np.ascontiguousarray(inputs[f"L1_gnn_{w}"])
    arrays["rel"] = np.ascontiguousarray(inputs["L2_gnn_weight"])
    for w in ("W1", "W2", "b2"):
        arrays[w] = np.ascontiguousarray(inputs[f"L3_gnn_{w}"])
    arrays["b1"] = np.ascontiguousarray(np.asarray(inputs["L3_gnn_b1"]).T)

    nc = _bacc.Bacc("TRN2", target_bir_lowering=False, num_devices=1)
    aps = {n: nc.dram_tensor(f"in_{n}", a.shape, mybir.dt.from_np(a.dtype), kind="ExternalInput").ap()
           for n, a in arrays.items()}
    out = nc.dram_tensor("out_x", (N, D), mybir.dt.float32, kind="ExternalOutput").ap()
    data = ["src", "typ", "wgt", "dst_row", "dst_prev", "dst_tile", "first", "edge_t", "x"]
    gnn_kernel(nc, *[aps[n] for n in data], {n: a for n, a in aps.items() if n not in data}, out)
    r = _run(nc, [{f"in_{n}": a for n, a in arrays.items()}], core_ids=[0])
    return r.results[0]["out_x"]
```

```python
from contextlib import ExitStack

import numpy as np

import concourse.bass as bass
from concourse import mybir

N, D, E, DE, R = 3125, 64, 103125, 32, 16
P = 128
TC = 4
EC = TC * P
C = -(-E // EC)
T = C * TC
EP = T * P
NB = -(-N // P)
NP = NB * P
NT = NP + P
GB = 4
GROUPS = [(b, min(GB, NB - b)) for b in range(0, NB, GB)]
G = len(GROUPS)
KA = D + DE + 1
U = 4
V = 2
BIG = 1e38
EPS = 1e-5


def gnn_kernel(nc, src, typ, wgt, dst_row, dst_prev, dst_tile, first, edge_t, x, W, out):
    f32, i32, bf16, f8 = mybir.dt.float32, mybir.dt.int32, mybir.dt.bfloat16, mybir.dt.float8e4
    u8 = mybir.dt.uint8
    ALU, ACT, AX = mybir.AluOpType, mybir.ActivationFunctionType, mybir.AxisListType

    SUM, ATT, REL, MAX = "sum", "att", "rel", "max"
    ROUNDS = [SUM, ATT, ATT, REL, MAX, MAX, MAX]
    NR = len(ROUNDS)

    def dram(name, shape, dt):
        return nc.dram_tensor(name, shape, dt).ap()

    srcs = [dram(f"src_table{r}", (NP * R if k == REL else NP, D), f32) for r, k in enumerate(ROUNDS)]
    width = [{ATT: KA, MAX: D}.get(k, 0) for k in ROUNDS]
    dsts = [dram(f"dst_table{r}", (NT, 3 * w), bf16) if w else None for r, w in enumerate(width)]
    onehots = dram("onehots", (C, P, 2 * EC), u8)
    states = [dram("states_sum", (EP, D), f32), dram("states_att", (EP, KA), f32)]

    ctx = ExitStack()
    with ctx:
        def sb(name, shape, dt=f32):
            return ctx.enter_context(nc.sbuf_tensor(name, shape, dt))

        def sem(name):
            return ctx.enter_context(nc.semaphore(name))

        ps = ctx.enter_context(nc.psum_tensor("ps", [P, 8, EC], f32))

        ident = sb("ident", [P, P])
        shift = sb("shift", [P, 2, P])
        eighth = sb("eighth", [P, P])
        iota_i = sb("iota_i", [P, NB], i32)
        node_id = sb("node_id", [P, NB])
        eps = sb("eps", [P, 1])
        zrow = sb("zrow", [P, 3 * KA], bf16)
        wq = [sb(f"wq{l}", [D + 1, D]) for l in range(2)]
        wkeb = [sb(f"wkeb{l}", [KA, D]) for l in range(2)]
        wqT = [sb(f"wqT{l}", [D, D + 1]) for l in range(2)]
        wkebT = [sb(f"wkebT{l}", [D, KA]) for l in range(2)]
        wquery = [sb(f"wquery{l}", [D + 1, KA]) for l in range(2)]
        wvalue = [sb(f"wvalue{l}", [KA, D]) for l in range(2)]
        wself = [sb(f"wself{l}", [D + 1, D]) for l in range(2)]
        wskip1 = sb("wskip1", [D + 1, D])
        wskip2 = sb("wskip2", [D, D])
        wrel = sb("wrel", [D, R, D])
        w1 = sb("w1", [D, 3, 2 * D])
        w1a = sb("w1a", [D, 3, D])
        w2 = sb("w2", [D, 3, D])
        b1 = sb("b1", [D, 3])
        b2 = sb("b2", [P, 3, D])

        src_i = sb("src_i", [P, T], i32)
        rel_i = sb("rel_i", [P, T], i32)
        wgt_sb = sb("wgt_sb", [P, T])
        first_i = sb("first_i", [P, T], i32)
        first_f = sb("first_f", [P, T])
        base = sb("base", [P, T])
        mask = sb("mask", [P, T])
        tiles_le = sb("tiles_le", [P, NB])
        tile_i = sb("tile_i", [P, NB], i32)
        within = sb("within", [P, NB])
        edges_le = sb("edges_le", [P, NB + 1])
        last_f = sb("last_f", [P, NB])
        last_i = sb("last_i", [P, NB], i32)
        deg = sb("deg", [P, NB])
        dinv = sb("dinv", [P, NB])

        xn = sb("xn", [P, NB, D])
        zn = sb("zn", [P, NB, D])
        agg = sb("agg", [P, NB, P])
        dst_rows = agg[:, :, :].bitcast(i32)
        xT = sb("xT", [D + 1, NP])
        hT = sb("hT", [D + 1, NP])
        gy = sb("gy", [P, V, GB, D])
        gx = sb("gx", [P, V, GB, D])
        gs = sb("gs", [P, V, GB, D])
        ga = sb("ga", [P, V, 8, GB])
        rT = sb("rT", [KA, V, EC])
        split_r = sb("split_r", [P, V, GB * KA])
        split3 = sb("split3", [P, V, GB * 3 * KA], bf16)
        rel_rows = sb("rel_rows", [P, V, R * D])

        idx = sb("idx", [P, U, TC], i32)
        nodes = sb("nodes", [P, U, TC])
        rows = sb("rows", [P, U, TC, D])
        sel = sb("sel", [P, U, 2 * EC], f8)
        win = sb("win", [P, U, TC, 3 * KA], bf16)
        dst_b = sb("dst_b", [P, U, EC], i32)
        prev_b = sb("prev_b", [P, U, EC], i32)
        xe = sb("xe", [KA, U, EC])
        prod = sb("prod", [KA, V, EC])
        pen = sb("pen", [KA, V, EC])
        runmax = sb("runmax", [KA, 1 + V * EC])
        diff = sb("diff", [KA, V, EC])
        decay = sb("decay", [KA, V, EC])
        msg = sb("msg", [KA, V, EC])
        st = sb("st", [KA, V, EC])
        hb = sb("hb", [P, U, TC * KA])

        def bank(n, s):
            return ps[:, V * n + s % V, :]
        TURNED, QUERY, SCORE, BACK = range(4)

        loaded = sem("loaded")
        dve_pre = sem("dve_pre")
        act_pre = sem("act_pre")
        pe_pre = sem("pe_pre")
        pool_pre = sem("pool_pre")
        dst_rows_ready = sem("dst_rows_ready")
        zeros_stored = sem("zeros_stored")
        out_stored = sem("out_stored")
        rel_pe, rel_act = sem("rel_pe"), sem("rel_act")
        agg_ready = [sem(f"agg_ready{g}") for g in range(G)]

        LN = ["sum", "mean", "centred", "square", "var", "rstd", "norm"]
        SPLIT_D, SPLIT_A = ["rest", "low"], ["high", "middle"]
        STEPS = {
            0: (["scaled", "added"] + LN + SPLIT_D, ["std", "xT"] + SPLIT_A, ["turn_x", "query"]),
            1: (["inv", "alpha"] + SPLIT_D, ["rT", "relu", "hT"] + SPLIT_A, ["turn_r", "conv", "turn_h", "query"]),
            2: (["inv", "alpha", "added"] + LN, ["rT", "relu", "h2T", "skip", "std", "xT"],
                ["turn_r", "conv", "turn_h", "skip", "turn_x"]),
            3: (["added"] + LN + SPLIT_D, ["std", "xT", "src"] + SPLIT_A, ["turn_x", "pq"]),
            4: (["biased", "relu"] + SPLIT_D, ["zT", "src"] + SPLIT_A, ["turn_z", "pq"]),
            5: (["biased", "relu"] + SPLIT_D, ["zT", "src"] + SPLIT_A, ["turn_z", "pq"]),
            6: (["biased", "relu", "added"] + LN, ["std"], []),
        }

        class Signal:
            def __init__(self, sem_, before):
                self.sem, self.before = sem_, before

        kept = {}

        def shared(name, per_round):
            s_, before = kept.get(name) or (sem(name), 0)
            kept[name] = (s_, before + per_round)
            return Signal(s_, before)

        class Round:
            def __init__(self, r, kind):
                self.r, self.kind = r, kind
                self.idx_ready = shared("idx_ready", C)
                self.turned = shared("turned", C)
                self.st_ready = shared("st_ready", C)
                self.back = shared("back", C)
                self.hb_ready = shared("hb_ready", C)
                if kind == SUM:
                    self.sel_made = shared("sel_made", C)
                    self.nodes_ready = shared("nodes_ready", C)
                if kind == REL:
                    self.weighted = shared("weighted", C)
                if kind in (MAX, ATT):
                    self.pen_ready = shared("pen_ready", C)
                if kind == MAX:
                    self.relu_ready = shared("relu_ready", C)
                    self.lifted = shared("lifted", C)
                if kind == ATT:
                    self.xe_ready = shared("xe_ready", C)
                    self.query_ready = shared("query_ready", C)
                    self.prod_ready = shared("prod_ready", C)
                    self.score_ready = shared("score_ready", C)
                    self.carry_ready = shared("carry_ready", -(-C // V))
                    self.max_ready = shared("max_ready", C)
                    self.diff_ready = shared("diff_ready", C)
                    self.before_ready = shared("before_ready", C)
                    self.ddecay_ready = shared("ddecay_ready", C)
                    self.exp_ready = shared("exp_ready", C)
                    self.decay_ready = shared("decay_ready", C)
                    self.msg_ready = shared("msg_ready", C)
                self.rows_ready = [sem(f"rows_ready_{r}_{s_}") for s_ in range(U)]
                self.in_ready = [sem(f"in_ready_{r}_{s_}") for s_ in range(U)]
                uses = [(C - s_ + U - 1) // U for s_ in range(U)]
                self.st_stored = [shared(f"st_stored_{s_}", 16 * uses[s_]) for s_ in range(U)]
                if kind == ATT:
                    self.edge_ready = [shared(f"edge_ready_{s_}", 16 * uses[s_]) for s_ in range(U)]
                self.src_stored = [sem(f"src_stored_{r}_{s_}") for s_ in range(V if kind == REL else 1)]
                self.dst_stored = [sem(f"dst_stored_{r}_{s_}") for s_ in range(V if width[r] else 0)]
                self.dve, self.act, self.pe = (shared(f"node_{e}", G * len(STEPS[r][i]))
                                               for i, e in enumerate(("dve", "act", "pe")))

        rounds = [Round(r, k) for r, k in enumerate(ROUNDS)]
        N_LOADS = 3 + 3 + 1 + 2 * (2 + 3 + 3 + 2) + 3 + 1 + 3 + 2
        PRE_POOL = 13

        def wait(eng, *pairs):
            found = []
            for s, value in pairs:
                if isinstance(value, int) and value <= 0:
                    continue
                if isinstance(s, Signal):
                    s, value = s.sem, value + s.before
                found.append((s, value if isinstance(value, int) else eng.to_reg(value)))
            if not all(isinstance(value, int) for _, value in found):
                eng.wait_ge(pool_pre, PRE_POOL)
            for s, value in found:
                eng.wait_ge(s, value)

        def sources_stored(q):
            if q.kind == REL:
                return [(q.src_stored[s], 16 * ((NB - s + V - 1) // V)) for s in range(V)]
            return [(q.src_stored[0], 16 * (G if q.r else 1))]

        def tables_stored(q):
            return sources_stored(q) + [(x, 16 * ((G - s + V - 1) // V)) for s, x in enumerate(q.dst_stored)]

        def chunks(eng, *stages):
            lags = [lag for lag, _ in stages]
            head = max(lags) + U

            def step(t, s, n):
                for lag, body in stages:
                    if not isinstance(t, int) or 0 <= t - lag < C:
                        body(t - lag, (s - lag) % U, n + (s - lag) // U)

            for t in range(head):
                step(t, t % U, t // U)
            loops = (C - head) // U
            with eng.Fori(0, loops) as i:
                for k in range(head, head + U):
                    step(U * i + k, k % U, i + k // U)
            for t in range(head + loops * U, C + max(lags)):
                step(t, t % U, t // U)

        def cols(c, k=1):
            return slice(c * k, c * k + k) if isinstance(c, int) else bass.ds(c * k, k)

        def at(steps, g, name):
            return len(steps) * g + steps.index(name) + 1

        sel_stored = [sem(f"sel_stored{s}") for s in range(U)]
        N_LOADS = 6 + 2 * 10 + 3 + 1 + 5
        PRE_POOL = 13

        def part(i, u, nb, w):
            return split3[:, u, 0:nb * 3 * w].rearrange("p (b i f) -> p b i f", i=3, f=w)[:, :, i, :]

        def blocks_of(psum, nb, w):
            return psum[:, 0:nb * w].rearrange("p (b f) -> p b f", f=w)

        def split_act(act, q, sa, sd, sp_, g, nb, w, psum, made):
            u = g % V
            wait(act, (q.pe, made))
            if g >= V:
                act.wait_ge(rounds[q.r + 1].dst_stored[u], 16 * (g // V))
            nc.scalar.activation(part(0, u, nb, w), psum, ACT.Copy).then_inc(q.act.sem, 1)
            wait(act, (q.dve, at(sd, g, "rest")))
            nc.scalar.activation(part(1, u, nb, w),
                                 split_r[:, u, 0:nb * w].rearrange("p (b f) -> p b f", f=w),
                                 ACT.Copy).then_inc(q.act.sem, 1)

        def split_dve(dve, q, sa, sd, g, nb, w, psum):
            u = g % V
            left = split_r[:, u, 0:nb * w].rearrange("p (b f) -> p b f", f=w)
            wait(dve, (q.act, at(sa, g, "high")))
            nc.vector.tensor_tensor(left, psum, part(0, u, nb, w), ALU.subtract).then_inc(q.dve.sem, 1)
            wait(dve, (q.act, at(sa, g, "middle")), (q.dve, at(sd, g, "rest")))
            nc.vector.tensor_tensor(part(2, u, nb, w), left, part(1, u, nb, w),
                                    ALU.subtract).then_inc(q.dve.sem, 1)

        def node_stores(sp, q):
            r = q.r
            sd, sa, _ = STEPS[r]
            nxt = rounds[r + 1] if r + 1 < NR else None
            for g, (b, nb) in enumerate(GROUPS):
                rows_of = slice(b * P, (b + nb) * P)
                if r in (0, 1, 3, 4, 5):
                    if r == 0:
                        wait(sp, (q.dve, at(sd, g, "norm")))
                        data = xn
                    elif r == 1:
                        wait(sp, (q.act, at(sa, g, "relu")))
                        data = zn
                    else:
                        wait(sp, (q.act, at(sa, g, "src")))
                        data = zn
                    sp.dma_start(srcs[r + 1][rows_of, :].rearrange("(b p) f -> p b f", p=P),
                                 data[:, b:b + nb, :]).then_inc(nxt.src_stored[0], 16)
                    w = width[r + 1]
                    wait(sp, (q.dve, at(sd, g, "low")))
                    sp.dma_start(dsts[r + 1][rows_of, :].rearrange("(b p) f -> p b f", p=P),
                                 split3[:, g % V, 0:nb * 3 * w].rearrange("p (b f) -> p b f", f=3 * w))\
                        .then_inc(nxt.dst_stored[g % V], 16)
                if r == 6:
                    wait(sp, (q.dve, at(sd, g, "norm")))
                    real = min((b + nb) * P, N) - b * P
                    if real == nb * P:
                        sp.dma_start(out[rows_of, :].rearrange("(b p) f -> p b f", p=P),
                                     xn[:, b:b + nb, :]).then_inc(out_stored, 16)
                    else:
                        whole = real // P
                        if whole:
                            sp.dma_start(out[b * P:(b + whole) * P, :].rearrange("(b p) f -> p b f", p=P),
                                         xn[:, b:b + whole, :]).then_inc(out_stored, 16)
                        else:
                            sp.sem_inc(out_stored, 16)
                        sp.dma_start(out[(b + whole) * P:N, :], xn[0:N - (b + whole) * P, b + whole, :])\
                            .then_inc(out_stored, 16)
            if r == 2:
                for b in range(NB):
                    sp.wait_ge(rel_act, b + 1)
                    sp.dma_start(srcs[3][b * P * R:(b + 1) * P * R, :].rearrange("(p r) f -> p (r f)", p=P),
                                 rel_rows[:, b % V, :]).then_inc(nxt.src_stored[b % V], 16)

        def node_act(act, q):
            r = q.r
            sd, sa, sp_ = STEPS[r]
            for g, (b, nb) in enumerate(GROUPS):
                u, n = g % V, nb * P

                def turned(dst, name, rows_n):
                    wait(act, (q.pe, at(sp_, g, name)))
                    nc.scalar.activation(dst, bank(0, u)[0:rows_n, 0:n], ACT.Copy).then_inc(q.act.sem, 1)

                def std():
                    wait(act, (q.dve, at(sd, g, "var")))
                    nc.scalar.activation(ga[:, u, 3, 0:nb], ga[:, u, 2, 0:nb], ACT.Sqrt, bias=eps[:, :],
                                         scale=1.0 / D).then_inc(q.act.sem, 1)

                if r == 0:
                    std()
                    turned(xT[0:D, b * P:b * P + n], "turn_x", D)
                    split_act(act, q, sa, sd, sp_, g, nb, KA, blocks_of(bank(1, u), nb, KA), at(sp_, g, "query"))
                elif r == 1:
                    turned(rT[0:KA, u, 0:n], "turn_r", KA)
                    wait(act, (q.pe, at(sp_, g, "conv")))
                    nc.scalar.activation(zn[:, b:b + nb, :], blocks_of(bank(1, u), nb, D), ACT.Relu)\
                        .then_inc(q.act.sem, 1)
                    turned(hT[0:D, b * P:b * P + n], "turn_h", D)
                    split_act(act, q, sa, sd, sp_, g, nb, KA, blocks_of(bank(2, u), nb, KA), at(sp_, g, "query"))
                elif r == 2:
                    turned(rT[0:KA, u, 0:n], "turn_r", KA)
                    wait(act, (q.pe, at(sp_, g, "conv")))
                    nc.scalar.activation(gy[:, u, 0:nb, :], blocks_of(bank(1, u), nb, D), ACT.Relu)\
                        .then_inc(q.act.sem, 1)
                    turned(rT[0:D, u, 0:n], "turn_h", D)
                    wait(act, (q.pe, at(sp_, g, "skip")))
                    nc.scalar.activation(gs[:, u, 0:nb, :], blocks_of(bank(2, u), nb, D), ACT.Relu)\
                        .then_inc(q.act.sem, 1)
                    std()
                    turned(xT[0:D, b * P:b * P + n], "turn_x", D)
                elif r in (3, 4, 5):
                    if r == 3:
                        std()
                    turned((xT if r == 3 else hT)[0:D, b * P:b * P + n], "turn_x" if r == 3 else "turn_z", D)
                    wait(act, (q.pe, at(sp_, g, "pq")))
                    if r > 3:
                        pass
                    pq = blocks_of(bank(1, u), nb, 2 * D)
                    nc.scalar.activation(zn[:, b:b + nb, :], pq[:, :, D:2 * D], ACT.Copy).then_inc(q.act.sem, 1)
                    split_act(act, q, sa, sd, sp_, g, nb, D, pq[:, :, 0:D], at(sp_, g, "pq"))
                else:
                    std()
            if r == 2:
                for b in range(NB):
                    act.wait_ge(rel_pe, b + 1)
                    if b >= V:
                        act.wait_ge(rounds[3].src_stored[b % V], 16 * (b // V))
                    nc.scalar.activation(rel_rows[:, b % V, :].rearrange("p (a f) -> p a f", a=2),
                                         ps[:, 2 * (b % V):2 * (b % V) + 2, :], ACT.Copy).then_inc(rel_act, 1)

        def node_pe(pe, q):
            r = q.r
            sd, sa, sp_ = STEPS[r]
            for g, (b, nb) in enumerate(GROUPS):
                u, n = g % V, nb * P

                def turn(src_of, w, value, sem_):
                    wait(pe, (sem_, value))
                    for j in range(nb):
                        last = nc.tensor.matmul(bank(0, u)[0:w, j * P:(j + 1) * P], src_of(j), ident[:, :],
                                                is_transpose=True, start=True, stop=True)
                    last.then_inc(q.pe.sem, 1)

                def product(psum, w, terms):
                    for j in range(nb):
                        for i, (lhs, rhs) in enumerate(terms):
                            last = nc.tensor.matmul(psum[:, j * w:(j + 1) * w], lhs(j), rhs,
                                                    start=i == 0, stop=i == len(terms) - 1)
                    last.then_inc(q.pe.sem, 1)

                def of(m, rows_n):
                    return lambda j: m[0:rows_n, (b + j) * P:(b + j + 1) * P]

                def of_group(rows_n):
                    return lambda j: rT[0:rows_n, u, j * P:(j + 1) * P]

                free0 = {0: "xT", 1: "hT", 2: "xT", 3: "xT", 4: "zT", 5: "zT"}.get(r)
                if g >= V and free0:
                    wait(pe, (q.act, at(sa, g - V, free0)))
                if r == 0:
                    turn(lambda j: xn[:, b + j, :], D, at(sd, g, "norm"), q.dve)
                    wait(pe, (q.act, at(sa, g, "xT")))
                    if g >= V:
                        wait(pe, (q.dve, at(sd, g - V, "rest")))
                    product(bank(1, u), KA, [(of(xT, D + 1), wquery[0][:, :])])
                elif r in (1, 2):
                    turn(lambda j: agg[:, b + j, 0:KA], KA, at(sd, g, "alpha"), q.dve)
                    wait(pe, (q.act, at(sa, g, "rT")))
                    product(bank(1, u), D, [(of_group(KA), wvalue[r - 1][:, :]),
                                            (of(xT if r == 1 else hT, D + 1), wself[r - 1][:, :])])
                    if r == 1:
                        turn(lambda j: zn[:, b + j, :], D, at(sa, g, "relu"), q.act)
                        wait(pe, (q.act, at(sa, g, "hT")))
                        if g >= V:
                            wait(pe, (q.dve, at(sd, g - V, "rest")))
                        product(bank(2, u), KA, [(of(hT, D + 1), wquery[1][:, :])])
                    else:
                        turn(lambda j: gy[:, u, j, :], D, at(sa, g, "relu"), q.act)
                        wait(pe, (q.act, at(sa, g, "h2T")))
                        product(bank(2, u), D, [(of(hT, D + 1), wskip1[:, :]), (of_group(D), wskip2[:, :])])
                        turn(lambda j: xn[:, b + j, :], D, at(sd, g, "norm"), q.dve)
                elif r in (3, 4, 5):
                    if r == 3:
                        turn(lambda j: xn[:, b + j, :], D, at(sd, g, "norm"), q.dve)
                    else:
                        turn(lambda j: zn[:, b + j, :], D, at(sd, g, "relu"), q.dve)
                    wait(pe, (q.act, at(sa, g, "xT" if r == 3 else "zT")))
                    if g >= V:
                        wait(pe, (q.dve, at(sd, g - V, "rest")), (q.act, at(sa, g - V, "high")))
                    product(bank(1, u), 2 * D, [(of(xT if r == 3 else hT, D), w1[:, r - 3, :])])
            if r == 2:
                wait(pe, (q.act, at(sa, G - 1, "xT")))
                for b in range(NB):
                    if b >= V:
                        pe.wait_ge(rel_act, b - V + 1)
                    for i in range(2):
                        last = nc.tensor.matmul(ps[:, 2 * (b % V) + i, :], xT[0:D, b * P:(b + 1) * P],
                                                wrel[:, i * R // 2:(i + 1) * R // 2, :].rearrange("d r o -> d (r o)"),
                                                start=True, stop=True)
                    last.then_inc(rel_pe, 1)

        def node_dve(dve, q):
            r = q.r
            sd, sa, sp_ = STEPS[r]
            for g, (b, nb) in enumerate(GROUPS):
                u = g % V
                y, xc, sq = gy[:, u, 0:nb, :], gx[:, u, 0:nb, :], gs[:, u, 0:nb, :]
                x_g, z_g, a_g = xn[:, b:b + nb, :], zn[:, b:b + nb, :], agg[:, b:b + nb, 0:D]
                small = lambda i: ga[:, u, i, 0:nb]
                wide = lambda v, w: v.unsqueeze(2).to_broadcast([P, nb, w])

                def op(name, ins):
                    ins.then_inc(q.dve.sem, 1)
                    wait(dve, (q.dve, at(sd, g, name)))

                def layer_norm(v):
                    op("sum", nc.vector.reduce_sum(small(0), v, axis=AX.X))
                    op("mean", nc.vector.tensor_scalar(small(1), small(0), -1.0 / D, None, ALU.mult))
                    op("centred", nc.vector.tensor_tensor(xc, v, wide(small(1), D), ALU.add))
                    op("square", nc.vector.tensor_tensor(sq, xc, xc, ALU.mult))
                    op("var", nc.vector.reduce_sum(small(2), sq, axis=AX.X))
                    wait(dve, (q.act, at(sa, g, "std")))
                    op("rstd", nc.vector.reciprocal(small(4), small(3)))
                    op("norm", nc.vector.tensor_tensor(x_g, xc, wide(small(4), D), ALU.mult))

                dve.wait_ge(agg_ready[g], 16 * nb * (r + 1))
                if r == 0:
                    op("scaled", nc.vector.tensor_tensor(y, a_g, wide(dinv[:, b:b + nb], D), ALU.mult))
                    op("added", nc.vector.tensor_tensor(y, y, x_g, ALU.add))
                    layer_norm(y)
                    split_dve(dve, q, sa, sd, g, nb, KA, blocks_of(bank(1, u), nb, KA))
                elif r in (1, 2):
                    a_k = agg[:, b:b + nb, 0:KA]
                    op("inv", nc.vector.reciprocal(small(0).unsqueeze(2), agg[:, b:b + nb, KA - 1:KA]))
                    op("alpha", nc.vector.tensor_tensor(a_k, a_k, wide(small(0), KA), ALU.mult))
                    if r == 1:
                        split_dve(dve, q, sa, sd, g, nb, KA, blocks_of(bank(2, u), nb, KA))
                    else:
                        wait(dve, (q.act, at(sa, g, "skip")))
                        op("added", nc.vector.tensor_tensor(y, sq, x_g, ALU.add))
                        layer_norm(y)
                elif r == 3:
                    op("added", nc.vector.scalar_tensor_tensor(y, a_g, 0.0, x_g, ALU.max, ALU.add))
                    layer_norm(y)
                    split_dve(dve, q, sa, sd, g, nb, D, blocks_of(bank(1, u), nb, 2 * D)[:, :, 0:D])
                else:
                    b2_l = b2[:, r - 4, :].unsqueeze(1).to_broadcast([P, nb, D])
                    op("biased", nc.vector.tensor_tensor(y, a_g, b2_l, ALU.add))
                    op("relu", nc.vector.tensor_scalar(z_g, y, 0.0, None, ALU.max))
                    if r < 6:
                        split_dve(dve, q, sa, sd, g, nb, D, blocks_of(bank(1, u), nb, 2 * D)[:, :, 0:D])
                    else:
                        op("added", nc.vector.tensor_tensor(y, z_g, x_g, ALU.add))
                        layer_norm(y)

        block = ctx.enter_context(nc.Block())

        @block.sync
        def _(sp):
            def load(dst, s):
                sp.dma_start(dst, s).then_inc(loaded, 16)

            load(first_i[:, :], first.to_broadcast([P, T]))
            load(src_i[:, :], src)
            load(rel_i[:, :], typ)
            load(wgt_sb[:, :], wgt)
            full = N // P
            load(xn[:, 0:full, :], x[0:full * P, :].rearrange("(b p) f -> p b f", p=P))
            for l in range(2):
                n = l + 1
                row = lambda name: W[name].rearrange("(a n) -> a n", a=1)
                load(wq[l][0:D, :], W[f"q{n}_w"])
                load(wq[l][D:D + 1, :], row(f"q{n}_b"))
                load(wkeb[l][0:D, :], W[f"k{n}_w"])
                load(wkeb[l][D:D + DE, :], W[f"e{n}_w"])
                load(wkeb[l][KA - 1:KA, :], row(f"k{n}_b"))
                load(wvalue[l][0:D, :], W[f"v{n}_w"])
                load(wvalue[l][D:D + DE, :], W[f"e{n}_w"])
                load(wvalue[l][KA - 1:KA, :], row(f"v{n}_b"))
                load(wself[l][0:D, :], W[f"s{n}_w"])
                load(wself[l][D:D + 1, :], row(f"s{n}_b"))
            load(wskip1[0:D, :], W["skip_w"][0:D, :])
            load(wskip1[D:D + 1, :], W["skip_b"].rearrange("(a n) -> a n", a=1))
            load(wskip2[:, :], W["skip_w"][D:2 * D, :])
            load(wrel[:, :, :], W["rel"].rearrange("r d o -> d r o"))
            load(w1a[:, :, :], W["W1"][:, 0:D, :].rearrange("l d o -> d l o"))
            load(w1[:, :, D:2 * D], W["W1"][:, D:2 * D, :].rearrange("l d o -> d l o"))
            load(w2[:, :, :], W["W2"].rearrange("l d o -> d l o"))
            load(b1[:, :], W["b1"])
            load(b2[:, :, :].rearrange("p l o -> p (l o)"),
                 W["b2"].rearrange("(a l) o -> a (l o)", a=1).to_broadcast([P, 3 * D]))
            sp.wait_ge(pool_pre, PRE_POOL)
            load(xn[0:N - full * P, full, :], x[full * P:N, :])
            for r in range(NR):
                if width[r]:
                    sp.dma_start(dsts[r][NP:NT, :], zrow[:, 0:3 * width[r]]).then_inc(zeros_stored, 16)
            sp.wait_ge(dve_pre, PRE_SCALED)
            sp.dma_start(srcs[0].rearrange("(b p) f -> p b f", p=P), zn[:, :, :]).then_inc(rounds[0].src_stored[0], 16)

            for q in rounds:
                r, k = q.r, q.kind
                kw = KA if k == ATT else D
                table = states[1] if k == ATT else states[0]

                def store_states(c, s, n):
                    wait(sp, (q.hb_ready, c + 1))
                    e = slice(c * EC, (c + 1) * EC) if isinstance(c, int) else bass.ds(c * EC, EC)
                    sp.dma_start(table[e, :].rearrange("(j p) f -> p j f", p=P),
                                 hb[:, s, 0:TC * kw].rearrange("p (j f) -> p j f", f=kw))\
                        .then_inc(q.st_stored[s].sem, 16)

                def one(c):
                    return c if isinstance(c, int) else bass.ds(c, 1)

                def fetch(c, s, n):
                    e = slice(c * EC, (c + 1) * EC) if isinstance(c, int) else bass.ds(c * EC, EC)
                    if k == SUM:
                        wait(sp, (q.sel_made, c - U + 1))
                        sp.dma_start(dst_b[:, s, :], dst_row[:, e].to_broadcast([P, EC])).then_inc(q.in_ready[s], 16)
                        sp.dma_start(prev_b[:, s, :], dst_prev[:, e].to_broadcast([P, EC])).then_inc(q.in_ready[s], 16)
                        return
                    used = [q.st_ready] if k == REL else [q.pen_ready, q.query_ready if k == ATT else q.turned]
                    wait(sp, *[(u, c - U + 1) for u in used])
                    o = onehots[one(c)]
                    o = o if isinstance(c, int) else o.rearrange("a p e -> (a p) e")
                    if k == REL:
                        sp.dma_start(sel[:, s, EC:].bitcast(u8), o[:, EC:]).then_inc(q.in_ready[s], 16)
                        return
                    sp.dma_start(sel[:, s, :].bitcast(u8), o).then_inc(q.in_ready[s], 16)
                    _, begins = nc.values_load_multi_w_load_instructions(
                        first_i[0:1, cols(c, TC)], engines=[mybir.EngineType.SP], min_val=0, max_val=NP)
                    for j in range(TC):
                        sp.dma_start(win[:, s, j, 0:3 * kw], dsts[r][bass.ds(begins[j], P), :]).then_inc(q.in_ready[s], 16)
                    if k == ATT:
                        wait(sp, (q.msg_ready, c - U + 1))
                        sp.dma_start(xe[D:D + DE, s, :], edge_t[:, e]).then_inc(q.edge_ready[s].sem, 16)

                def store_onehots(c, s, n):
                    wait(sp, (q.sel_made, c + 1))
                    o = onehots[one(c)]
                    o = o if isinstance(c, int) else o.rearrange("a p e -> (a p) e")
                    sp.dma_start(o, sel[:, s, :].bitcast(u8)).then_inc(sel_stored[s], 16)

                if r == 0:
                    pass
                else:
                    if r == 1:
                        for s in range(U):
                            sp.wait_ge(sel_stored[s], 16 * ((C - s + U - 1) // U))
                        sp.wait_ge(zeros_stored, 16 * sum(w > 0 for w in width))
                    wait(sp, *tables_stored(q))
                stages = [(0, fetch)] + [(2, store_onehots)] * (k == SUM) + [(U, store_states)]
                chunks(sp, *stages)
                node_stores(sp, q)
            sp.wait_ge(out_stored, 16 * (G + 1))

        @block.gpsimd
        def _(pool):
            pool.memset(ident[:, :], 0.0).then_inc(pool_pre, 1)
            pool.memset(shift[:, :, :], 0.0).then_inc(pool_pre, 1)
            pool.memset(eighth[:, :], float(D) ** -0.5).then_inc(pool_pre, 1)
            pool.memset(zrow[:, :], 0.0).then_inc(pool_pre, 1)
            pool.memset(eps[:, :], EPS).then_inc(pool_pre, 1)
            pool.memset(xT[:, :], 1.0).then_inc(pool_pre, 1)
            pool.memset(hT[:, :], 1.0).then_inc(pool_pre, 1)
            pool.memset(xe[:, :, :], 1.0).then_inc(pool_pre, 1)
            pool.memset(xn[:, NB - 1, :], 0.0).then_inc(pool_pre, 1)
            nc.gpsimd.iota(iota_i[:, :], pattern=[[P, NB]], base=0, channel_multiplier=1).then_inc(pool_pre, 1)
            pool.wait_ge(pool_pre, 2)
            nc.gpsimd.affine_select(out=ident[:, :], in_=ident[:, :], compare_op=ALU.not_equal, fill=1.0,
                                    base=0, pattern=[[-1, P]], channel_multiplier=1).then_inc(pool_pre, 1)
            nc.gpsimd.affine_select(out=shift[:, 0, :], in_=shift[:, 0, :], compare_op=ALU.not_equal, fill=1.0,
                                    base=1, pattern=[[-1, P]], channel_multiplier=1).then_inc(pool_pre, 1)
            nc.gpsimd.affine_select(out=shift[:, 1, :], in_=shift[:, 1, :], compare_op=ALU.not_equal, fill=1.0,
                                    base=-(P - 1), pattern=[[-1, P]], channel_multiplier=1).then_inc(pool_pre, 1)

            pool.wait_ge(dve_pre, PRE_TILES)
            for b in range(NB):
                pool.indirect_dma_start(dst_rows[:, b, :], None, dst_tile,
                                        bass.IndirectOffsetOnAxis(ap=tile_i[:, b:b + 1], axis=0))\
                    .then_inc(dst_rows_ready, 16)

            for q in rounds:
                def gather(c, s, n):
                    wait(pool, *sources_stored(q), (q.idx_ready, c + 1), (q.turned, c - U + 1))
                    for j in range(TC):
                        pool.indirect_dma_start(rows[:, s, j, :], None, srcs[q.r],
                                                bass.IndirectOffsetOnAxis(ap=idx[:, s, j:j + 1], axis=0))\
                            .then_inc(q.rows_ready[s], 16)
                chunks(pool, (0, gather))
                kw = KA if q.kind == ATT else D
                for s in range(U):
                    wait(pool, (q.st_stored[s], 16 * ((C - s + U - 1) // U)))
                for g, (b0, nb) in enumerate(GROUPS):
                    for b in range(b0, b0 + nb):
                        pool.indirect_dma_start(agg[:, b, 0:kw], None, states[1] if q.kind == ATT else states[0],
                                                bass.IndirectOffsetOnAxis(ap=last_i[:, b:b + 1], axis=0))\
                            .then_inc(agg_ready[g], 16)

        @block.scalar
        def _(act):
            act.wait_ge(pool_pre, PRE_POOL)
            for l in range(2):
                act.wait_ge(pe_pre, 2 * l + 2)
                nc.scalar.activation(wqT[l][:, :], bank(0, l)[0:D, 0:D + 1], ACT.Copy).then_inc(act_pre, 1)
                nc.scalar.activation(wkebT[l][:, :], bank(0, l)[0:D, P:P + KA], ACT.Copy).then_inc(act_pre, 1)
            act.wait_ge(pe_pre, 6)
            for l in range(2):
                nc.scalar.activation(wquery[l][:, :], bank(1, l)[0:D + 1, 0:KA], ACT.Copy).then_inc(act_pre, 1)
            act.wait_ge(dve_pre, PRE_DEG)
            nc.scalar.activation(deg[:, :], deg[:, :], ACT.Sqrt).then_inc(act_pre, 1)

            for q in rounds:
                k = q.kind
                kw = KA if k == ATT else D

                def indices(c, s, n):
                    if k == SUM:
                        wait(act, (q.sel_made, c - U + 1))
                        nc.scalar.activation(nodes[:, s, :], base[:, cols(c, TC)], ACT.Copy).then_inc(q.nodes_ready.sem, 1)
                    wait(act, (q.rows_ready[s], 64 * n))
                    src_idx = rel_i if k == REL else src_i
                    nc.scalar.activation(idx[:, s, :], src_idx[:, cols(c, TC)], ACT.Copy).then_inc(q.idx_ready.sem, 1)

                def penalty(c, s, n):
                    wait(act, (q.in_ready[s], 16 * (TC + 1) * (n + 1)),
                         (q.before_ready if k == ATT else q.st_ready, c - V + 1))
                    nc.scalar.activation(pen[0:kw, s % V, :], sel[0:kw, s, EC:], ACT.Copy, scale=BIG, bias=-BIG)\
                        .then_inc(q.pen_ready.sem, 1)

                def states_out(c, s, n):
                    wait(act, (q.back, c + 1), (q.st_stored[s], 16 * n))
                    nc.scalar.activation(hb[:, s, 0:TC * kw], bank(BACK, s)[:, 0:TC * kw], ACT.Copy)\
                        .then_inc(q.hb_ready.sem, 1)

                def exponentials(c, s, n):
                    wait(act, (q.diff_ready, c + 1))
                    nc.scalar.activation(diff[:, s % V, :], diff[:, s % V, :], ACT.Exp).then_inc(q.exp_ready.sem, 1)
                    wait(act, (q.ddecay_ready, c + 1))
                    nc.scalar.activation(decay[:, s % V, :], decay[:, s % V, :], ACT.Exp).then_inc(q.decay_ready.sem, 1)

                def features(c, s, n):
                    if k == ATT:
                        wait(act, (q.turned, c + 1), (q.msg_ready, c - U + 1))
                        nc.scalar.activation(xe[0:D, s, :], bank(TURNED, s)[0:D, :], ACT.Copy)\
                            .then_inc(q.xe_ready.sem, 1)
                    else:
                        wait(act, (q.turned, c + 1), (q.lifted, c - U + 1))
                        nc.scalar.activation(xe[0:D, s, :], bank(TURNED, s)[0:D, :], ACT.Relu,
                                             bias=b1[:, q.r - 4:q.r - 3]).then_inc(q.relu_ready.sem, 1)

                if k == ATT:
                    chunks(act, (U, features), (0, indices), (U, penalty), (U + 2, exponentials),
                           (U + 3, states_out))
                elif k == MAX:
                    chunks(act, (U, features), (0, indices), (U, penalty), (U + 2, states_out))
                else:
                    chunks(act, (0, indices), (U + 1, states_out))
                node_act(act, q)

        @block.tensor
        def _(pe):
            pe.wait_ge(pool_pre, PRE_POOL)
            pe.wait_ge(loaded, 16 * N_LOADS)
            for l in range(2):
                nc.tensor.transpose(bank(0, l)[0:D, 0:D + 1], wq[l][:, :], ident[0:D + 1, 0:D + 1]).then_inc(pe_pre, 1)
                nc.tensor.transpose(bank(0, l)[0:D, P:P + KA], wkeb[l][:, :], ident[0:KA, 0:KA]).then_inc(pe_pre, 1)
            pe.wait_ge(act_pre, 4)
            for l in range(2):
                nc.tensor.matmul(bank(1, l)[0:D + 1, 0:KA], wqT[l][:, :], wkebT[l][:, :], start=True, stop=True)\
                    .then_inc(pe_pre, 1)
            pe.wait_ge(dve_pre, PRE_EDGES)
            nc.tensor.matmul(bank(2, 0)[:, 0:NB], shift[:, 0, :], edges_le[:, 1:NB + 1], start=True, stop=False)
            nc.tensor.matmul(bank(2, 0)[:, 0:NB], shift[:, 1, :], edges_le[:, 0:NB], start=False, stop=True)\
                .then_inc(pe_pre, 1)

            for q in rounds:
                k = q.kind
                kw = KA if k == ATT else D

                def turn(c, s, n):
                    made = {REL: [(q.weighted, c + 1)] if k == REL else [],
                            MAX: [(q.in_ready[s], 16 * (TC + 1) * (n + 1))]}.get(k, [])
                    emptied = q.xe_ready if k == ATT else q.relu_ready if k == MAX else q.st_ready
                    wait(pe, (q.rows_ready[s], 64 * (n + 1)), *made, (emptied, c - V + 1))
                    for j in range(TC):
                        o = bank(TURNED, s)[0:D, j * P:(j + 1) * P]
                        last = nc.tensor.matmul(o, rows[:, s, j, :], ident[:, :], is_transpose=True,
                                                start=True, stop=k != MAX)
                        if k == MAX:
                            for i in range(3):
                                last = nc.tensor.matmul(o, win[:, s, j, i * kw:(i + 1) * kw],
                                                        sel[:, s, j * P:(j + 1) * P], start=False, stop=i == 2)
                    last.then_inc(q.turned.sem, 1)

                def query(c, s, n):
                    wait(pe, (q.in_ready[s], 16 * (TC + 1) * (n + 1)), (q.prod_ready, c - V + 1))
                    for j in range(TC):
                        for i in range(3):
                            last = nc.tensor.matmul(bank(QUERY, s)[0:KA, j * P:(j + 1) * P],
                                                    win[:, s, j, i * KA:(i + 1) * KA],
                                                    sel[:, s, j * P:(j + 1) * P], start=i == 0, stop=i == 2)
                    last.then_inc(q.query_ready.sem, 1)

                def score(c, s, n):
                    wait(pe, (q.prod_ready, c + 1), (q.diff_ready, c - V + 1))
                    nc.tensor.matmul(bank(SCORE, s)[0:KA, :], eighth[0:KA, 0:KA], prod[:, s % V, :],
                                     start=True, stop=True).then_inc(q.score_ready.sem, 1)

                def lift(c, s, n):
                    wait(pe, (q.relu_ready, c + 1), (q.st_ready, c - V + 1))
                    nc.tensor.matmul(bank(QUERY, s)[0:D, :], w2[:, q.r - 4, :], xe[0:D, s, :],
                                     start=True, stop=True).then_inc(q.lifted.sem, 1)

                def back(c, s, n):
                    wait(pe, (q.st_ready, c + 1), (q.hb_ready, c - V + 1))
                    for j in range(TC):
                        last = nc.tensor.matmul(bank(BACK, s)[:, j * kw:(j + 1) * kw],
                                                st[0:kw, s % V, j * P:(j + 1) * P], ident[0:kw, 0:kw],
                                                is_transpose=True, start=True, stop=True)
                    last.then_inc(q.back.sem, 1)

                if k == ATT:
                    chunks(pe, (0, turn), (0, query), (1, score), (3, back))
                elif k == MAX:
                    chunks(pe, (0, turn), (1, lift), (2, back))
                else:
                    chunks(pe, (0, turn), (1, back))
                node_pe(pe, q)

        @block.vector
        def _(dve):
            made = [0]

            def pre(ins):
                made[0] += 1
                ins.then_inc(dve_pre, 1)
                dve.wait_ge(dve_pre, made[0])

            dve.wait_ge(pool_pre, PRE_POOL)
            dve.wait_ge(loaded, 16 * N_LOADS)
            pre(nc.vector.tensor_copy(node_id[:, :], iota_i[:, :]))
            pre(nc.vector.tensor_copy(first_f[:, :], first_i[:, :]))
            pre(nc.vector.tensor_scalar(base[:, :], first_f[:, :], node_id[:, 0:1], None, ALU.add))
            for b in range(NB):
                pre(nc.vector.tensor_scalar(mask[:, :], first_f[:, :], node_id[:, b:b + 1], None, ALU.is_le))
                pre(nc.vector.reduce_sum(tiles_le[:, b:b + 1], mask[:, :], axis=AX.X))
            pre(nc.vector.tensor_scalar(tiles_le[:, :], tiles_le[:, :], -1.0, 0.0, ALU.add, ALU.max))
            pre(nc.vector.tensor_copy(tile_i[:, :], tiles_le[:, :]))
            assert made[0] == PRE_TILES
            pre(nc.vector.memset(edges_le[:, 0:1], 0.0))
            pre(nc.vector.tensor_scalar(mask[:, :], src_i[:, :], float(R), None, ALU.mult))
            pre(nc.vector.tensor_tensor(mask[:, :], mask[:, :], rel_i[:, :], ALU.add))
            pre(nc.vector.tensor_copy(rel_i[:, :], mask[:, :]))
            pre(nc.vector.tensor_tensor(w1[:, :, 0:D], w1a[:, :, :], w1[:, :, D:2 * D], ALU.subtract))
            dve.wait_ge(dst_rows_ready, 16 * NB)
            pre(nc.vector.tensor_tensor(agg[:, :, :], dst_rows, node_id[:, :].unsqueeze(2).to_broadcast([P, NB, P]),
                                        ALU.is_le))
            pre(nc.vector.reduce_sum(within[:, :], agg[:, :, :], axis=AX.X))
            pre(nc.vector.scalar_tensor_tensor(edges_le[:, 1:NB + 1], tiles_le[:, :], float(P), within[:, :],
                                               ALU.mult, ALU.add))
            assert made[0] == PRE_EDGES
            pre(nc.vector.tensor_scalar(last_f[:, :], edges_le[:, 1:NB + 1], -1.0, 0.0, ALU.add, ALU.max))
            pre(nc.vector.tensor_copy(last_i[:, :], last_f[:, :]))
            dve.wait_ge(pe_pre, 7)
            pre(nc.vector.tensor_tensor(deg[:, :], edges_le[:, 1:NB + 1], bank(2, 0)[:, 0:NB], ALU.subtract))
            pre(nc.vector.tensor_scalar(deg[:, :], deg[:, :], 1.0, None, ALU.max))
            assert made[0] == PRE_DEG
            dve.wait_ge(act_pre, 7)
            pre(nc.vector.reciprocal(dinv[:, :], deg[:, :]))
            pre(nc.vector.tensor_tensor(zn[:, :, :], xn[:, :, :], dinv[:, :].unsqueeze(2).to_broadcast([P, NB, D]),
                                        ALU.mult))
            assert made[0] == PRE_SCALED

            for q in rounds:
                k = q.kind
                kw = KA if k == ATT else D

                def scan(c, s, d0, d1, op0, op1):
                    wait(dve, (q.back, c - V + 1), (q.st_ready, c))
                    first_one = isinstance(c, int) and c == 0
                    init = (0.0 if op1 == ALU.add else -BIG) if first_one else st[0:kw, (s - 1) % V, EC - 1:EC]
                    nc.vector.tensor_tensor_scan(st[0:kw, s % V, :], d0, d1, init, op0, op1).then_inc(q.st_ready.sem, 1)

                def make_onehots(c, s, n):
                    wait(dve, (q.in_ready[s], 32 * (n + 1)), (q.nodes_ready, c + 1), (sel_stored[s], 16 * n))
                    nc.vector.tensor_tensor(sel[:, s, EC:], dst_b[:, s, :], prev_b[:, s, :], ALU.is_equal,
                                            saturate=False)
                    for j in range(TC):
                        last = nc.vector.tensor_scalar(sel[:, s, j * P:(j + 1) * P], dst_b[:, s, j * P:(j + 1) * P],
                                                       nodes[:, s, j:j + 1], None, ALU.is_equal, saturate=False)
                    last.then_inc(q.sel_made.sem, 1)

                def step_plain(c, s, n):
                    if k == SUM:
                        make_onehots(c, s, n)
                        wait(dve, (q.sel_made, c + 1))
                    if k == REL:
                        wait(dve, (q.rows_ready[s], 64 * (n + 1)))
                        nc.vector.tensor_tensor(rows[:, s, :, :], rows[:, s, :, :],
                                                wgt_sb[:, cols(c, TC)].unsqueeze(2).to_broadcast([P, TC, D]),
                                                ALU.mult).then_inc(q.weighted.sem, 1)
                        wait(dve, (q.in_ready[s], 16 * (n + 1)))
                    if k == MAX:
                        wait(dve, (q.lifted, c + 1), (q.pen_ready, c + 1))
                        scan(c, s, pen[0:D, s % V, :], bank(QUERY, s)[0:D, :], ALU.add, ALU.max)
                    else:
                        wait(dve, (q.turned, c + 1))
                        scan(c, s, sel[0:D, s, EC:], bank(TURNED, s)[0:D, :], ALU.mult, ALU.add)

                def product(c, s, n):
                    wait(dve, (q.query_ready, c + 1),
                         (q.xe_ready, c + 1),
                         (q.edge_ready[s], 16 * (n + 1)),
                         (q.score_ready, c - V + 1))
                    nc.vector.tensor_tensor(prod[:, s % V, :], bank(QUERY, s)[0:KA, :], xe[:, s, :], ALU.mult)\
                        .then_inc(q.prod_ready.sem, 1)

                def accumulate(c, s, n):
                    wait(dve, (q.exp_ready, c + 1), (q.xe_ready, c + 1))
                    nc.vector.tensor_tensor(msg[:, s % V, :], diff[:, s % V, :], xe[:, s, :], ALU.mult)\
                        .then_inc(q.msg_ready.sem, 1)
                    wait(dve, (q.decay_ready, c + 1), (q.msg_ready, c + 1))
                    scan(c, s, decay[:, s % V, :], msg[:, s % V, :], ALU.mult, ALU.add)

                def maxima(c, s, n):
                    v = s % V
                    m = runmax[:, 1 + v * EC:1 + (v + 1) * EC]
                    before = runmax[:, v * EC:(v + 1) * EC]
                    if isinstance(c, int) and c == 0:
                        nc.vector.memset(runmax[:, 0:1], -BIG).then_inc(q.carry_ready.sem, 1)
                        wait(dve, (q.carry_ready, 1))
                    elif v == 0:
                        wait(dve, (q.max_ready, c))
                        nc.vector.tensor_copy(runmax[:, 0:1], runmax[:, V * EC:V * EC + 1]).then_inc(q.carry_ready.sem, 1)
                        wait(dve, (q.carry_ready, n * (U // V) + s // V + 1))
                    wait(dve, (q.max_ready, c), (q.score_ready, c + 1), (q.pen_ready, c + 1))
                    nc.vector.tensor_tensor_scan(m, pen[:, s % V, :], bank(SCORE, s)[0:KA, :], before[:, 0:1],
                                                 ALU.add, ALU.max).then_inc(q.max_ready.sem, 1)
                    wait(dve, (q.max_ready, c + 1), (q.msg_ready, c - V + 1))
                    nc.vector.tensor_tensor(diff[:, s % V, :], bank(SCORE, s)[0:KA, :], m, ALU.subtract)\
                        .then_inc(q.diff_ready.sem, 1)
                    wait(dve, (q.st_ready, c - V + 1))
                    nc.vector.tensor_tensor(decay[:, s % V, :], before, pen[:, s % V, :], ALU.add).then_inc(q.before_ready.sem, 1)
                    wait(dve, (q.before_ready, c + 1))
                    nc.vector.tensor_tensor(decay[:, s % V, :], decay[:, s % V, :], m, ALU.subtract)\
                        .then_inc(q.ddecay_ready.sem, 1)

                if k == ATT:
                    chunks(dve, (0, product), (2, accumulate), (1, maxima))
                else:
                    chunks(dve, (0, step_plain))
                node_dve(dve, q)

_WEIGHTS = ["q1_w", "q1_b", "k1_w", "k1_b", "v1_w", "v1_b", "e1_w", "s1_w", "s1_b", "q2_w", "q2_b", "k2_w",
            "k2_b", "v2_w", "v2_b", "e2_w", "s2_w", "s2_b", "skip_w", "skip_b"]

PRE_TILES = 3 + 2 * NB + 2
PRE_EDGES = PRE_TILES + 5 + 3
PRE_DEG = PRE_EDGES + 4
PRE_SCALED = PRE_DEG + 2


def kernel(**inputs):
    import concourse.bacc as _bacc
    from concourse.bass_utils import run_bass_kernel_spmd as _run

    def padded(a, value):
        a = np.asarray(a).reshape(-1)
        return np.concatenate([a, np.full(EP - E, value, a.dtype)])

    def tiled(a, value):
        return np.ascontiguousarray(padded(a, value).reshape(T, P).T)

    dst = padded(inputs["dst"], N)
    edge = np.asarray(inputs["edge_attr_32"])
    arrays = {
        "src": tiled(inputs["src"], 0),
        "typ": tiled(inputs["edge_type_16"], 0),
        "wgt": tiled(inputs["edge_weight1"], 0),
        "dst_row": dst.reshape(1, EP),
        "dst_prev": np.concatenate([np.full(1, -1, dst.dtype), dst[:-1]]).reshape(1, EP),
        "dst_tile": dst.reshape(T, P),
        "first": np.ascontiguousarray(dst[::P]).reshape(1, T),
        "edge_t": np.ascontiguousarray(np.concatenate([edge, np.zeros((EP - E, DE), edge.dtype)]).T),
        "x": np.ascontiguousarray(inputs["x"]),
    }
    for w in _WEIGHTS:
        arrays[w] = np.ascontiguousarray(inputs[f"L1_gnn_{w}"])
    arrays["rel"] = np.ascontiguousarray(inputs["L2_gnn_weight"])
    for w in ("W1", "W2", "b2"):
        arrays[w] = np.ascontiguousarray(inputs[f"L3_gnn_{w}"])
    arrays["b1"] = np.ascontiguousarray(np.asarray(inputs["L3_gnn_b1"]).T)

    nc = _bacc.Bacc("TRN2", target_bir_lowering=False, num_devices=1)
    aps = {n: nc.dram_tensor(f"in_{n}", a.shape, mybir.dt.from_np(a.dtype), kind="ExternalInput").ap()
           for n, a in arrays.items()}
    out = nc.dram_tensor("out_x", (N, D), mybir.dt.float32, kind="ExternalOutput").ap()
    data = ["src", "typ", "wgt", "dst_row", "dst_prev", "dst_tile", "first", "edge_t", "x"]
    gnn_kernel(nc, *[aps[n] for n in data], {n: a for n, a in aps.items() if n not in data}, out)
    r = _run(nc, [{f"in_{n}": a for n, a in arrays.items()}], core_ids=[0])
    return r.results[0]["out_x"]
```
